# Optimizing a Trainium2 kernel written in Bass

```python
import numpy as np
import jax
import jax.numpy as jnp

def _softmax(x, axis=-1):
    return jax.nn.softmax(x, axis=axis)

def _gelu(x):
    return jax.nn.gelu(x, approximate=True)

def _silu(x):
    return jax.nn.silu(x)

def _sigmoid(x):
    return jax.nn.sigmoid(x)

def _layernorm(x, axis=-1, eps=1e-05):
    m = jnp.mean(x, axis=axis, keepdims=True)
    v = jnp.var(x, axis=axis, keepdims=True)
    return (x - m) / jnp.sqrt(v + eps)

def _scatter_add(tgt, idx, src, axis=0):
    return tgt.at[idx].add(src)

def _segment_sum(src, seg, n):
    return jax.ops.segment_sum(src, seg, n)
kernel_name = 'mk_macaron_d1_jaxref_r4_9441e4'

def setup_inputs(seed: int=0):
    np.random.seed(seed)
    _w = jnp.asarray

    def _L0_attn_setup():
        import jax, jax.numpy as jnp
        import numpy as np
        DIM = 256
        NUM_HEADS = 16
        HEAD_DIM = DIM // NUM_HEADS
        B, L = (4, 512)

        def _alibi_bias_causal(seq_len, dtype):
            h = jnp.arange(1, NUM_HEADS + 1, dtype=jnp.float32)
            slopes = jnp.power(2.0, -8.0 * h / NUM_HEADS)
            pos = jnp.arange(seq_len, dtype=jnp.float32)
            rel = jnp.abs(pos[:, None] - pos[None, :])
            bias = -slopes[:, None, None] * rel[None, :, :]
            causal = pos[:, None] >= pos[None, :]
            bias = jnp.where(causal[None, :, :], bias, -jnp.inf)
            return bias.astype(dtype)
        key = jax.random.key(seed)
        ks = jax.random.split(key, 9)
        s = 0.02
        return {'x': jax.random.normal(ks[0], (B, L, DIM), jnp.float32), 'Wq': jax.random.normal(ks[1], (DIM, DIM), jnp.float32) * s, 'bq': jax.random.normal(ks[2], (DIM,), jnp.float32) * s, 'Wk': jax.random.normal(ks[3], (DIM, DIM), jnp.float32) * s, 'bk': jax.random.normal(ks[4], (DIM,), jnp.float32) * s, 'Wv': jax.random.normal(ks[5], (DIM, DIM), jnp.float32) * s, 'bv': jax.random.normal(ks[6], (DIM,), jnp.float32) * s, 'Wo': jax.random.normal(ks[7], (DIM, DIM), jnp.float32) * s, 'bo': jax.random.normal(ks[8], (DIM,), jnp.float32) * s}
    _L0_attn_in = _L0_attn_setup()

    def _L0_ffn_setup():
        import jax, jax.numpy as jnp
        import numpy as np
        B, S, D, O, E, K = (4, 512, 256, 256, 8, 2)
        key = jax.random.key(seed)
        ks = jax.random.split(key, 5)
        scale_in = 1.0 / np.sqrt(D)
        x = jax.random.normal(ks[0], (B, S, D), dtype=jnp.float32)
        gate_w = jax.random.uniform(ks[1], (E, D), jnp.float32, -scale_in, scale_in)
        gate_b = jax.random.uniform(ks[2], (E,), jnp.float32, -scale_in, scale_in)
        expert_w = jax.random.uniform(ks[3], (E, D, O), jnp.float32, -scale_in, scale_in)
        expert_b = jax.random.uniform(ks[4], (E, O), jnp.float32, -scale_in, scale_in)
        return {'x': x, 'gate_w': gate_w, 'gate_b': gate_b, 'expert_w': expert_w, 'expert_b': expert_b}
    _L0_ffn_in = _L0_ffn_setup()
    _d = {'L0_attn_x': _L0_attn_in['x'], 'L0_attn_Wq': _L0_attn_in['Wq'], 'L0_attn_bq': _L0_attn_in['bq'], 'L0_attn_Wk': _L0_attn_in['Wk'], 'L0_attn_bk': _L0_attn_in['bk'], 'L0_attn_Wv': _L0_attn_in['Wv'], 'L0_attn_bv': _L0_attn_in['bv'], 'L0_attn_Wo': _L0_attn_in['Wo'], 'L0_attn_bo': _L0_attn_in['bo'], 'L0_ffn_gate_w': _L0_ffn_in['gate_w'], 'L0_ffn_gate_b': _L0_ffn_in['gate_b'], 'L0_ffn_expert_w': _L0_ffn_in['expert_w'], 'L0_ffn_expert_b': _L0_ffn_in['expert_b']}
    _x0 = _d['L0_attn_x']
    _d['L0_attn_x'] = jax.random.normal(jax.random.fold_in(jax.random.key(seed), 1), (1, 4096, 256), dtype=_x0.dtype)
    del _x0
    return _d

def reference(L0_attn_x, L0_attn_Wq, L0_attn_bq, L0_attn_Wk, L0_attn_bk, L0_attn_Wv, L0_attn_bv, L0_attn_Wo, L0_attn_bo, L0_ffn_gate_w, L0_ffn_gate_b, L0_ffn_expert_w, L0_ffn_expert_b):

    def _L0_attn_ref(x, Wq, bq, Wk, bk, Wv, bv, Wo, bo):
        import jax, jax.numpy as jnp
        import numpy as np
        DIM = 256
        NUM_HEADS = 16
        HEAD_DIM = DIM // NUM_HEADS
        B, L = (4, 512)

        def _alibi_bias_causal(seq_len, dtype):
            h = jnp.arange(1, NUM_HEADS + 1, dtype=jnp.float32)
            slopes = jnp.power(2.0, -8.0 * h / NUM_HEADS)
            pos = jnp.arange(seq_len, dtype=jnp.float32)
            rel = jnp.abs(pos[:, None] - pos[None, :])
            bias = -slopes[:, None, None] * rel[None, :, :]
            causal = pos[:, None] >= pos[None, :]
            bias = jnp.where(causal[None, :, :], bias, -jnp.inf)
            return bias.astype(dtype)
        b, l, d = x.shape
        q = (jnp.einsum('bld,ed->ble', x, Wq) + bq).reshape(b, l, NUM_HEADS, HEAD_DIM).transpose(0, 2, 1, 3)
        k = (jnp.einsum('bld,ed->ble', x, Wk) + bk).reshape(b, l, NUM_HEADS, HEAD_DIM).transpose(0, 2, 1, 3)
        v = (jnp.einsum('bld,ed->ble', x, Wv) + bv).reshape(b, l, NUM_HEADS, HEAD_DIM).transpose(0, 2, 1, 3)
        scale = 1.0 / np.sqrt(HEAD_DIM)
        scores = jnp.einsum('bhqd,bhkd->bhqk', q, k) * scale
        scores = scores + _alibi_bias_causal(l, scores.dtype)[None]
        attn = jax.nn.softmax(scores, axis=-1)
        out = jnp.einsum('bhqk,bhkd->bhqd', attn, v)
        out = out.transpose(0, 2, 1, 3).reshape(b, l, d)
        return jnp.einsum('bld,ed->ble', out, Wo) + bo

    def _L0_ffn_ref(x, gate_w, gate_b, expert_w, expert_b):
        import jax, jax.numpy as jnp
        import numpy as np
        B, S, D, O, E, K = (4, 512, 256, 256, 8, 2)
        logits = jnp.einsum('bsd,ed->bse', x, gate_w) + gate_b
        if K < E:
            topv, topi = jax.lax.top_k(logits, K)
            keep = jax.nn.one_hot(topi, E, dtype=jnp.float32).sum(axis=-2)
            logits = jnp.where(keep > 0, logits, -jnp.inf)
        gate_score = jax.nn.softmax(logits, axis=-1)
        expert_out = jnp.einsum('bsd,edo->bseo', x, expert_w) + expert_b
        out = jnp.einsum('bseo,bse->bso', expert_out, gate_score)
        return out
    x = L0_attn_x
    x = x + 0.5 * _L0_ffn_ref(_layernorm(x, axis=-1), L0_ffn_gate_w, L0_ffn_gate_b, L0_ffn_expert_w, L0_ffn_expert_b)
    x = x + _L0_attn_ref(_layernorm(x, axis=-1), L0_attn_Wq, L0_attn_bq, L0_attn_Wk, L0_attn_bk, L0_attn_Wv, L0_attn_bv, L0_attn_Wo, L0_attn_bo)
    x = x + 0.5 * _L0_ffn_ref(_layernorm(x, axis=-1), L0_ffn_gate_w, L0_ffn_gate_b, L0_ffn_expert_w, L0_ffn_expert_b)
    return x

_drawn_inputs = setup_inputs


def setup_inputs(seed=0):
    import zlib

    import numpy as np

    out = dict(_drawn_inputs(seed))
    spreads = {}
    factors = {'L0_attn_Wq': 7.123,
     'L0_attn_bq': 26.235,
     'L0_attn_Wk': 6.857,
     'L0_attn_bk': 64.0,
     'L0_attn_bv': 3.995}
    for name, (base, spread) in spreads.items():
        noise = np.random.default_rng([zlib.crc32(name.encode()), seed]).standard_normal(out[name].shape)
        drawn = base * np.exp(spread * noise) if base else spread * noise
        out[name] = jnp.asarray(drawn.astype(out[name].dtype))
    for name, factor in factors.items():
        out[name] = (out[name] * factor).astype(out[name].dtype)
    return out
```

```python
from contextlib import ExitStack

import numpy as np
import concourse.bass as bass
from concourse import mybir

fp32 = mybir.dt.float32
f32r = mybir.dt.float32r
bf16 = mybir.dt.bfloat16
ALU = mybir.AluOpType
ACT = mybir.ActivationFunctionType
AX = mybir.AxisListType
ds = bass.ds


class Named:
    pass


L, D = 4096, 256
H, HD = 16, 16
E = 8
P = 128
KD = D // P
GT = 4
GW = GT * P
NG = L // GW
EPB = 512 // D
NB = E // EPB
EPS = 1e-5

QB = 512
NQB = L // QB
HG = 4
NHG = H // HG
KR = 96
AR = 6
MR = 2
Q_PART = (0, 1, 0, 1, 2, 0)
K_PART = (0, 0, 1, 1, 0, 2)
NEG = -1.0e30
CW = 2 * NQB - 1


def constant_arrays():
    def cut(v):
        return (np.ascontiguousarray(v, np.float32).view(np.uint32) & 0xFFFF0000).view(np.float32)

    def half(v):
        bits = np.ascontiguousarray(v, np.float32).view(np.uint32)
        assert not (bits & 0xFFFF).any()
        return (bits >> 16).astype(np.uint16)

    slope = np.power(np.float32(2.0), (-8.0 * np.arange(1, H + 1, dtype=np.float32) / H)).astype(np.float32)
    s1 = cut(slope)
    s2 = cut(slope - s1)
    s3 = cut(slope - s1 - s2)
    parts = np.stack([s1, s2, s3, s1, s2, s3])
    k = np.arange(L)
    k_rows = np.ones((AR + MR, L), np.float32)
    k_rows[0:3] = k % 256
    k_rows[3:6] = 256 * ((k // 256) % 2)
    q_rows = np.zeros((AR + MR, H, QB), np.float32)
    q_rows[0:AR] = parts[:, :, None]
    m_parts = np.zeros((NHG, HG, 4, AR + MR), np.float32)
    m_parts[..., 0:AR] = parts.T.reshape(NHG, HG, 1, AR)
    m_parts = np.broadcast_to(m_parts.reshape(1, -1), (P, NHG * 16 * 8))
    off = slope[:, None] * (np.float32(QB) * (np.arange(CW, dtype=np.float32) - (NQB - 1)))[None, :]
    p = np.arange(P)
    tri = (p[None, :E] < p[:E, None]).astype(np.float32)
    return {
        "c_ident": np.eye(P, dtype=np.float32),
        "c_ident16": half(np.eye(P)),
        "c_tri": np.broadcast_to(tri.reshape(1, E * E), (P, E * E)).copy(),
        "c_mask_q": half(cut(np.where(p[None, :] <= p[:, None], 0.0, NEG))),
        "c_mask_k": half(cut(np.where(p[None, :] >= p[:, None], 0.0, NEG))),
        "c_off": np.broadcast_to(off.reshape(1, H * CW), (P, H * CW)).astype(np.float32).copy(),
        "c_mparts": half(m_parts),
        "c_krows": half(k_rows),
        "c_qrows": half(q_rows.reshape(AR + MR, H * QB)),
    }


def plan_memory(nc):
    m = Named()
    at = [(nc.sbuf_base + 31) // 32 * 32]

    def put(name, cols, dt, parts=P):
        size = cols * (2 if dt == bf16 else 4)
        t = nc.alloc_sbuf_tensor_at(name, [parts, cols], dt, offset=at[0])
        at[0] += (size + 31) // 32 * 32
        return t

    m.ident = put("ident", P, fp32)
    m.ident16 = put("ident16", P, bf16)
    m.tri = put("tri", E * E, fp32)
    m.mask_q = put("mask_q", P, bf16)
    m.mask_k = put("mask_k", P, bf16)
    m.off = put("off", H * CW, fp32)
    m.mparts = put("mparts", NHG * 16 * 8, bf16)
    m.zero16 = put("zero16", 512, bf16)
    m.eps = put("eps", 1, fp32)
    base = at[0]

    m.xs = put("xs", NG * GT * D, fp32)
    m.w_raw = put("w_raw", KD * E * D, fp32)
    m.w_hi = put("w_hi", KD * E * D, f32r)
    m.w_lo = put("w_lo", KD * E * D, f32r)
    m.g_raw = put("g_raw", KD * E, fp32)
    m.g_hi = put("g_hi", KD * E, f32r)
    m.g_lo = put("g_lo", KD * E, f32r)
    m.gb = put("gb", 1, fp32)
    m.eb = put("eb", D, fp32)
    m.xh = [put(f"xh{u}", GT * D, fp32) for u in range(2)]
    m.xt_hi = [put(f"xt_hi{u}", KD * GW, f32r) for u in range(2)]
    m.xt_lo = [put(f"xt_lo{u}", KD * GW, f32r) for u in range(2)]
    m.bst = put("bst", GT * 6, fp32)
    m.mv = [put(f"mv{u}", GT * 2, fp32) for u in range(2)]
    m.std = put("std", GT, fp32)
    m.rstd = put("rstd", GT, fp32)
    m.lgt = put("lgt", GW, fp32)
    m.lg = put("lg", GT * E, fp32)
    m.top = put("top", GT, fp32)
    m.dl = put("dl", GT * E, fp32)
    m.ex = put("ex", GT * E, fp32)
    m.gtr = put("gtr", GT * E * E, fp32)
    m.eqr = put("eqr", GT * E * E, fp32)
    m.rank = put("rank", GT * E, fp32)
    m.gsum = put("gsum", GT, fp32)
    m.grec = put("grec", GT, fp32)
    m.gates = [put(f"gates{u}", GT * E, fp32) for u in range(2)]
    m.gts = [put(f"gts{u}", GW, fp32) for u in range(2)]
    m.acc = [put(f"acc{i}", D, fp32) for i in range(2)]
    after_ffn = at[0]
    m.qkv_raw = put("qkv_raw", KD * 3 * D, fp32)
    m.qkv_hi = put("qkv_hi", KD * 3 * D, f32r)
    m.qkv_lo = put("qkv_lo", KD * 3 * D, f32r)
    m.qk_bias = put("qk_bias", 4, fp32)
    m.v_bias = put("v_bias", D, fp32)
    m.tq = [put(f"tq{i}", GW, fp32) for i in range(2)]
    m.tr = [put(f"tr{i}", GW, fp32) for i in range(2)]
    m.parts = [put(f"parts{i}", 3 * GW, bf16) for i in range(2)]
    m.vpad = [put(f"vpad{u}", GT * H * 32, fp32) for u in range(2)]
    end_a = at[0]
    at[0] = after_ffn
    m.wo_raw = put("wo_raw", NHG * D, fp32)
    m.wo_hi = put("wo_hi", NHG * D, f32r)
    m.wo_lo = put("wo_lo", NHG * D, f32r)
    m.at_raw = [put(f"at_raw{u}", NHG * GW, fp32) for u in range(2)]
    m.at_hi = put("at_hi", NHG * GW, f32r)
    m.at_lo = put("at_lo", NHG * GW, f32r)
    end_c = at[0]
    at[0] = base
    m.K = put("K", H * L, bf16)
    m.Q = put("Q", H * QB, bf16)
    m.prob = [put(f"prob{p}", HG * 2 * QB, fp32) for p in range(2)]
    m.V = [put(f"V{p}", 2 * P, fp32) for p in range(2)]
    m.o = [put(f"o{i}", QB, fp32) for i in range(2)]
    m.rden = put("rden", QB, fp32)
    m.sums = put("sums", HG * QB // P, fp32)
    m.recips = put("recips", HG * QB // P, fp32)
    m.pm = [put(f"pm{i}", 16 * NQB, fp32) for i in range(2)]
    m.pmo = [put(f"pmo{i}", 16 * (NQB + 1), fp32) for i in range(2)]
    m.nmax = put("nmax", 16, fp32)
    end_b = at[0]
    assert max(end_a, end_b, end_c) <= nc.sbuf_usable_end, (end_a, end_b, end_c)
    return m


def program(nc, ins, out, stages=4, dbg=None):
    ctx = ExitStack()
    with ctx:
        m = plan_memory(nc)
        bank = [ctx.enter_context(nc.psum_tensor(f"bank{i}", [P, 512], fp32)) for i in range(4)]
        pair = [ctx.enter_context(nc.psum_tensor(f"pair{i}", [P, 1024], fp32)) for i in range(2)]
        exb = [pair[0][:, 0:512], pair[0][:, 512:1024], pair[1][:, 0:512], pair[1][:, 512:1024]]
        tb = [bank[0], bank[1]]
        gb = bank[2]
        rb = bank[3]
        mb = [bank[0], bank[1], bank[3]]
        ob = bank[2]
        xb = bank[3]

        def scratch(name, shape, dt):
            return nc.dram_tensor(name, shape, dt, kind="Internal").ap()

        x1_d = scratch("x1_d", [L, D], fp32)
        qk_d = scratch("qk_d", [2, 3, D, L], bf16)
        v_d = scratch("v_d", [NHG, L // P, P, P], fp32)
        at_d = scratch("at_d", [NHG, P, L], fp32)
        sums_d = scratch("sums_d", [HG, QB], fp32)
        recips_d = scratch("recips_d", [HG, QB], fp32)

        def sem(name):
            return ctx.enter_context(nc.semaphore(name))

        consts_in = sem("consts_in")
        ones_set = sem("ones_set")
        phase_end = sem("phase_end")

        def norm_sems(k):
            s = Named()
            s.stats = sem(f"{k}_stats")
            s.std = sem(f"{k}_std")
            s.rstd = sem(f"{k}_rstd")
            s.xhat = sem(f"{k}_xhat")
            s.turned = sem(f"{k}_turned")
            s.hi = sem(f"{k}_hi")
            s.lo = sem(f"{k}_lo")
            return s

        def ffn_sems(k):
            s = norm_sems(k)
            s.w_in = sem(f"{k}_w_in")
            s.w_hi = sem(f"{k}_w_hi")
            s.w_lo = sem(f"{k}_w_lo")
            s.lgt = sem(f"{k}_lgt")
            s.lgt_copied = sem(f"{k}_lgt_copied")
            s.lg = sem(f"{k}_lg")
            s.soft = sem(f"{k}_soft")
            s.shifted = sem(f"{k}_shifted")
            s.ex = sem(f"{k}_ex")
            s.gates = sem(f"{k}_gates")
            s.gt = sem(f"{k}_gt")
            s.gt_copied = sem(f"{k}_gt_copied")
            s.bias = sem(f"{k}_bias")
            s.acc_set = sem(f"{k}_acc_set")
            s.experts = sem(f"{k}_experts")
            s.used = sem(f"{k}_used")
            s.added = sem(f"{k}_added")
            s.stored0 = sem(f"{k}_stored0")
            s.stored1 = sem(f"{k}_stored1")
            s.x_in0 = sem(f"{k}_x_in0")
            s.x_in1 = sem(f"{k}_x_in1")
            return s

        f1 = ffn_sems("f1")
        f2 = ffn_sems("f2")
        f2.wo_in = sem("f2_wo_in")
        f2.wo_hi = sem("f2_wo_hi")
        f2.wo_lo = sem("f2_wo_lo")
        f2.wo_set = sem("f2_wo_set")
        f2.at_in0 = sem("f2_at_in0")
        f2.at_in1 = sem("f2_at_in1")
        f2.at_hi = sem("f2_at_hi")
        f2.at_lo = sem("f2_at_lo")
        f2.attended = sem("f2_attended")
        f2.x2 = sem("f2_x2")
        pj = norm_sems("pj")
        pj.w_in = sem("pj_w_in")
        pj.w_hi = sem("pj_w_hi")
        pj.w_lo = sem("pj_w_lo")
        pj.qk = sem("pj_qk")
        pj.qk_copied = sem("pj_qk_copied")
        pj.split = sem("pj_split")
        pj.part1 = sem("pj_part1")
        pj.part2 = sem("pj_part2")
        pj.part3 = sem("pj_part3")
        pj.parts_out0 = sem("pj_parts_out0")
        pj.parts_out1 = sem("pj_parts_out1")
        pj.v = sem("pj_v")
        pj.v_copied = sem("pj_v_copied")
        pj.v_out0 = sem("pj_v_out0")
        pj.v_out1 = sem("pj_v_out1")
        a = Named()
        a.k_in = sem("a_k_in")
        a.st = sem("a_st")
        a.exp = sem("a_exp")
        a.pv = sem("a_pv")
        a.m = sem("a_m")
        a.mx = sem("a_mx")
        a.fin = sem("a_fin")
        a.mp = sem("a_mp")
        a.mt = sem("a_mt")
        a.qrow = sem("a_qrow")
        a.o_copied = sem("a_o_copied")
        a.sums_out = sem("a_sums_out")
        a.sums_in = sem("a_sums_in")
        a.recips_out = sem("a_recips_out")
        a.recips_in = sem("a_recips_in")
        a.recip = sem("a_recip")
        a.normed = sem("a_normed")
        a.at_out0 = sem("a_at_out0")
        a.at_out1 = sem("a_at_out1")
        a.v_in0 = sem("a_v_in0")
        a.v_in1 = sem("a_v_in1")
        a.rows_in = sem("a_rows_in")
        a.pm_set = sem("a_pm_set")
        a.q_in0 = sem("a_q_in0")
        a.q_in1 = sem("a_q_in1")
        a.q_in2 = sem("a_q_in2")
        a.q_in3 = sem("a_q_in3")
        a.q_in = [a.q_in0, a.q_in1, a.q_in2, a.q_in3]
        a.v_in = [a.v_in0, a.v_in1]
        a.at_out = [a.at_out0, a.at_out1]

        S = Named()
        S.nc = nc
        S.m = m
        S.ins = ins
        S.out = out
        S.exb = exb
        S.tb = tb
        S.gb = gb
        S.rb = rb
        S.mb = mb
        S.ob = ob
        S.xb = xb
        S.es = pair
        S.x1_d = x1_d
        S.qk_d = qk_d
        S.v_d = v_d
        S.at_d = at_d
        S.sums_d = sums_d
        S.recips_d = recips_d
        S.f1 = f1
        S.f2 = f2
        S.pj = pj
        S.a = a
        S.wait_value = {}
        S.consts_in = consts_in
        S.ones_set = ones_set
        S.phase_end = phase_end

        block = ctx.enter_context(nc.Block())

        def phases(eng, name, parts):
            S.wait_value[eng] = eng.alloc_register(f"{name}_wait_value")
            for n, part in enumerate(parts[:stages]):
                if n:
                    eng.wait_ge(phase_end, 5 * n)
                part(eng, S)
                if n < stages - 1:
                    eng.drain().then_inc(phase_end, 1)

        @block.sync
        def _(sp):
            phases(sp, "sp", [ffn1_dma, project_dma, attend_dma, ffn2_dma])

        @block.tensor
        def _(pe):
            phases(pe, "pe", [ffn1_pe, project_pe, attend_pe, ffn2_pe])

        @block.scalar
        def _(act):
            phases(act, "act", [ffn1_act, project_act, attend_act, ffn2_act])

        @block.vector
        def _(dve):
            phases(dve, "dve", [ffn1_dve, project_dve, attend_dve, ffn2_dve])

        @block.gpsimd
        def _(pool):
            phases(pool, "pool", [ffn1_pool, project_pool, attend_pool, ffn2_pool])


def wait_alone(eng, S, sem, value):
    if isinstance(value, int):
        eng.wait_ge(sem, value)
        return
    eng.reg_mov(S.wait_value[eng], value)
    eng.wait_ge(S.consts_in, 16)
    eng.wait_ge(sem, S.wait_value[eng])



def norm_stats_dve(dve, S, s, G, u, ready):
    m = S.m
    ready()
    for t in range(GT):
        dve.bn_stats(m.bst[:, 6 * t:6 * t + 6], m.xs[:, ds((G * GT + t) * D, D)]).then_inc(s.stats, 1)
    wait_alone(dve, S, s.stats, 2 * GT * G + GT)
    for t in range(GT):
        dve.bn_aggr(m.mv[u][:, 2 * t:2 * t + 2], m.bst[:, 6 * t:6 * t + 6]).then_inc(s.stats, 1)


def norm_std_act(act, S, s, G, u):
    m = S.m
    act.wait_ge(s.stats, 2 * GT * G + 2 * GT)
    act.activation(m.std[:, :], m.mv[u][:, 1:2 * GT:2], ACT.Sqrt, bias=m.eps[:, :]).then_inc(s.std, 1)


def norm_apply_dve(dve, S, s, G, u):
    m = S.m
    dve.wait_ge(s.std, G + 1)
    dve.reciprocal(m.rstd[:, :], m.std[:, :]).then_inc(s.rstd, 1)
    dve.wait_ge(s.rstd, G + 1)
    if not (isinstance(G, int) and G < 2):
        dve.wait_ge(s.turned, KD * (G - 1))
    for t in range(GT):
        dve.tensor_scalar(m.xh[u][:, t * D:(t + 1) * D], m.xs[:, ds((G * GT + t) * D, D)],
                          m.mv[u][:, 2 * t:2 * t + 1], m.rstd[:, t:t + 1], ALU.subtract, ALU.mult).then_inc(s.xhat, 1)


def turn_pe(pe, S, s, G, u, free):
    m = S.m
    pe.wait_ge(s.xhat, GT * (G + 1))
    free()
    for k in range(KD):
        for t in range(GT):
            last = pe.transpose(S.tb[k][:, t * P:(t + 1) * P], m.xh[u][:, t * D + k * P:t * D + (k + 1) * P],
                                m.ident[:, :])
        last.then_inc(s.turned, 1)


def turn_hi_act(act, S, s, G, u, free):
    m = S.m
    free()
    for k in range(KD):
        act.wait_ge(s.turned, KD * G + k + 1)
        act.activation(m.xt_hi[u][:, k * GW:(k + 1) * GW], S.tb[k][:, :], ACT.Copy).then_inc(s.hi, 1)


def turn_lo_dve(dve, S, s, G, u):
    m = S.m
    for k in range(KD):
        dve.wait_ge(s.hi, KD * G + k + 1)
        dve.tensor_tensor(m.xt_lo[u][:, k * GW:(k + 1) * GW], S.tb[k][:, :],
                          m.xt_hi[u][:, k * GW:(k + 1) * GW].bitcast(fp32), ALU.subtract).then_inc(s.lo, 1)


def split_product(pe, out, hi, lo, w_hi, w_lo, tiles):
    n = 3 * len(tiles)
    i = 0
    for k in tiles:
        for lhs, rhs in ((hi(k), w_hi(k)), (lo(k), w_hi(k)), (hi(k), w_lo(k))):
            last = pe.matmul(out, lhs, rhs, start=(i == 0), stop=(i == n - 1))
            i += 1
    return last



def groups(eng, body):
    body(0, 0, True, True)
    body(1, 1, True, True)
    with eng.Fori(1, NG // 2 - 1) as gp:
        body(2 * gp, 0, True, True)
        body(2 * gp + 1, 1, True, True)
    body(NG - 2, 0, True, False)
    body(NG - 1, 1, False, False)


def load_expert_weights(sp, S, s):
    m, ins = S.m, S.ins
    sp.dma_start(m.g_raw[:, :].rearrange("p (k e) -> p k e", k=KD),
                 ins["gate_wT"].rearrange("(k p) e -> p k e", p=P)).then_inc(s.w_in, 16)
    sp.dma_start(m.gb[0:E, :], ins["gate_b"].rearrange("(e a) -> e a", a=1)).then_inc(s.w_in, 16)
    sp.dma_start(m.eb[0:E, :], ins["expert_b"]).then_inc(s.w_in, 16)
    for k in range(KD):
        sp.dma_start(m.w_raw[:, k * E * D:(k + 1) * E * D].rearrange("p (e o) -> p e o", e=E),
                     ins["expert_w"][:, k * P:(k + 1) * P, :].rearrange("e p o -> p e o")).then_inc(s.w_in, 16)


W_LOADS = 16 * (3 + KD)


def split_weights_act(act, S, s):
    m = S.m
    act.wait_ge(s.w_in, W_LOADS)
    act.activation(m.g_hi[:, :], m.g_raw[:, :], ACT.Copy).then_inc(s.w_hi, 1)
    act.activation(m.w_hi[:, :], m.w_raw[:, :], ACT.Copy).then_inc(s.w_hi, 1)


def split_weights_dve(dve, S, s):
    m = S.m
    dve.wait_ge(s.w_hi, 2)
    dve.tensor_tensor(m.g_lo[:, :], m.g_raw[:, :], m.g_hi[:, :].bitcast(fp32), ALU.subtract).then_inc(s.w_lo, 1)
    dve.tensor_tensor(m.w_lo[:, :], m.w_raw[:, :], m.w_hi[:, :].bitcast(fp32), ALU.subtract).then_inc(s.w_lo, 1)


def logits_pe(pe, S, s, G, u):
    m = S.m
    pe.wait_ge(s.lo, KD * (G + 1))
    if not (isinstance(G, int) and G == 0):
        pe.wait_ge(s.gt_copied, G)
    split_product(pe, S.gb[0:E, :],
                  lambda k: m.g_hi[:, k * E:(k + 1) * E], lambda k: m.g_lo[:, k * E:(k + 1) * E],
                  lambda k: m.xt_hi[u][:, k * GW:(k + 1) * GW], lambda k: m.xt_lo[u][:, k * GW:(k + 1) * GW],
                  range(KD)).then_inc(s.lgt, 1)


def logits_copy_act(act, S, s, G):
    act.wait_ge(s.lgt, G + 1)
    act.activation(S.m.lgt[0:E, :], S.gb[0:E, :], ACT.Identity, bias=S.m.gb[0:E, :]).then_inc(s.lgt_copied, 1)


def logits_turn_pe(pe, S, s, G):
    wait_alone(pe, S, s.lgt_copied, G + 1)
    for t in range(GT):
        last = pe.transpose(S.gb[:, t * E:(t + 1) * E], S.m.lgt[0:E, t * P:(t + 1) * P], S.m.ident[0:E, 0:E])
    last.then_inc(s.lg, 1)


def gates_dve(dve, S, s, G, u):
    m = S.m
    own = 10 * G
    dve.wait_ge(s.lg, G + 1)
    dve.tensor_copy(m.lg[:, :], S.gb[:, 0:GT * E]).then_inc(s.soft, 1)
    lg = m.lg[:, :].rearrange("p (t e) -> p t e", t=GT)
    dve.wait_ge(s.soft, own + 1)
    dve.tensor_reduce(m.top[:, :], lg, axis=AX.X, op=ALU.max).then_inc(s.soft, 1)
    other = lg.unsqueeze(2).broadcast_to([P, GT, E, E])
    this = lg.unsqueeze(3).broadcast_to([P, GT, E, E])
    gtr = m.gtr[:, :].rearrange("p (t e f) -> p t e f", t=GT, e=E)
    eqr = m.eqr[:, :].rearrange("p (t e f) -> p t e f", t=GT, e=E)
    tri = m.tri[:, :].rearrange("p (e f) -> p e f", e=E).unsqueeze(1).broadcast_to([P, GT, E, E])
    dve.wait_ge(s.soft, own + 2)
    dve.tensor_tensor(m.dl[:, :].rearrange("p (t e) -> p t e", t=GT), lg,
                      m.top[:, :].unsqueeze(2).broadcast_to([P, GT, E]), ALU.subtract).then_inc(s.shifted, 1)
    dve.tensor_tensor(eqr, other, this, ALU.is_equal).then_inc(s.soft, 1)
    dve.tensor_tensor(gtr, other, this, ALU.is_gt).then_inc(s.soft, 1)
    dve.wait_ge(s.soft, own + 3)
    dve.tensor_tensor(eqr, eqr, tri, ALU.mult).then_inc(s.soft, 1)
    dve.wait_ge(s.soft, own + 5)
    dve.tensor_tensor(m.gtr[:, :], m.gtr[:, :], m.eqr[:, :], ALU.add).then_inc(s.soft, 1)
    dve.wait_ge(s.soft, own + 6)
    dve.tensor_reduce(m.rank[:, :], gtr, axis=AX.X, op=ALU.add).then_inc(s.soft, 1)
    dve.wait_ge(s.soft, own + 7)
    dve.wait_ge(s.ex, G + 1)
    dve.scalar_tensor_tensor(m.rank[:, :], m.rank[:, :], 1.5, m.ex[:, :], ALU.is_lt, ALU.mult).then_inc(s.soft, 1)
    dve.wait_ge(s.soft, own + 8)
    rank = m.rank[:, :].rearrange("p (t e) -> p t e", t=GT)
    dve.tensor_reduce(m.gsum[:, :], rank, axis=AX.X, op=ALU.add).then_inc(s.soft, 1)
    dve.wait_ge(s.soft, own + 9)
    dve.reciprocal(m.grec[:, :], m.gsum[:, :]).then_inc(s.soft, 1)
    dve.wait_ge(s.soft, own + 10)
    dve.scalar_tensor_tensor(m.gates[u][:, :].rearrange("p (t e) -> p t e", t=GT), rank, 0.5,
                             m.grec[:, :].unsqueeze(2).broadcast_to([P, GT, E]), ALU.mult, ALU.mult).then_inc(s.gates, 1)


def gates_exp_act(act, S, s, G):
    act.wait_ge(s.shifted, G + 1)
    act.activation(S.m.ex[:, :], S.m.dl[:, :], ACT.Exp).then_inc(s.ex, 1)


def gates_turn_pe(pe, S, s, G, u):
    pe.wait_ge(s.gates, G + 1)
    for t in range(GT):
        last = pe.transpose(S.gb[0:E, t * P:(t + 1) * P], S.m.gates[u][:, t * E:(t + 1) * E], S.m.ident[:, :])
    last.then_inc(s.gt, 1)


def gates_copy_act(act, S, s, G, u):
    act.wait_ge(s.gt, G + 1)
    if not (isinstance(G, int) and G == 0):
        act.wait_ge(s.bias, GT * (G - 1))
    act.activation(S.m.gts[u][0:E, :], S.gb[0:E, :], ACT.Copy).then_inc(s.gt_copied, 1)


def experts_pe(pe, S, s, G, u, t):
    m = S.m
    T = G * GT + t
    if t == 0:
        pe.wait_ge(s.gt_copied, G + 1)
    if not (isinstance(T, int) and T == 0):
        pe.wait_ge(s.acc_set, T)
    pe.matmul(S.rb[:, 0:D], m.gts[u][0:E, t * P:(t + 1) * P], m.eb[0:E, :], start=True, stop=True).then_inc(s.bias, 1)
    for n in range(NB):
        pe.wait_ge(s.used, E * T + EPB * (n + 1))
        split_product(pe, S.exb[n],
                      lambda k: m.xt_hi[u][:, k * GW + t * P:k * GW + (t + 1) * P],
                      lambda k: m.xt_lo[u][:, k * GW + t * P:k * GW + (t + 1) * P],
                      lambda k: m.w_hi[:, k * E * D + n * 512:k * E * D + (n + 1) * 512],
                      lambda k: m.w_lo[:, k * E * D + n * 512:k * E * D + (n + 1) * 512],
                      range(KD)).then_inc(s.experts, 1)


def bias_act(act, S, s, G, t):
    T = G * GT + t
    act.wait_ge(s.bias, T + 1)
    act.wait_ge(s.added, T + 1)
    act.activation(S.m.acc[t % 2][:, :], S.rb[:, 0:D], ACT.Copy).then_inc(s.acc_set, 1)


def experts_dve(dve, S, s, G, u, t):
    m = S.m
    T = G * GT + t
    x = m.xs[:, ds(T * D, D)]
    acc = m.acc[t % 2][:, :]
    dve.wait_ge(s.acc_set, T + 1)
    for n in range(NB):
        dve.wait_ge(s.experts, NB * T + n + 1)
        for i, into in enumerate((x, acc)):
            e = EPB * n + i
            if n:
                dve.wait_ge(s.used, E * T + E + e - 1)
            dve.scalar_tensor_tensor(into, S.exb[n][:, i * D:(i + 1) * D], m.gates[u][:, t * E + e:t * E + e + 1],
                                     into, ALU.mult, ALU.add).then_inc(s.used, 1)


def add_pool(pool, S, s, G, t):
    T = G * GT + t
    x = S.m.xs[:, ds(T * D, D)]
    pool.wait_ge(s.used, E * T + 2 * E)
    pool.tensor_tensor(x, x, S.m.acc[t % 2][:, :], ALU.add).then_inc(s.added, 1)


def ffn_pe(pe, S, s, before, free_tb, also):
    turn_pe(pe, S, s, 0, 0, lambda: free_tb(0))
    pe.wait_ge(s.w_lo, 2)
    logits_pe(pe, S, s, 0, 0)
    logits_turn_pe(pe, S, s, 0)
    gates_turn_pe(pe, S, s, 0, 0)

    def body(G, u, nxt, nxt2):
        experts_pe(pe, S, s, G, u, 0)
        if nxt:
            turn_pe(pe, S, s, G + 1, 1 - u, lambda: free_tb(G + 1))
        experts_pe(pe, S, s, G, u, 1)
        if nxt:
            logits_pe(pe, S, s, G + 1, 1 - u)
        experts_pe(pe, S, s, G, u, 2)
        if nxt:
            logits_turn_pe(pe, S, s, G + 1)
        experts_pe(pe, S, s, G, u, 3)
        if nxt:
            gates_turn_pe(pe, S, s, G + 1, 1 - u)
        if nxt2:
            also(G + 2, u)

    groups(pe, body)


def ffn_act(act, S, s, also):
    def free_xt(G):
        if not (isinstance(G, int) and G == 0):
            act.wait_ge(s.experts, GT * NB * (G - 1))
    turn_hi_act(act, S, s, 0, 0, lambda: free_xt(0))
    logits_copy_act(act, S, s, 0)
    gates_exp_act(act, S, s, 0)
    gates_copy_act(act, S, s, 0, 0)

    def body(G, u, nxt, nxt2):
        bias_act(act, S, s, G, 0)
        if nxt:
            turn_hi_act(act, S, s, G + 1, 1 - u, lambda: free_xt(G + 1))
        if nxt2:
            also(G + 2, u)
        bias_act(act, S, s, G, 1)
        if nxt:
            logits_copy_act(act, S, s, G + 1)
        bias_act(act, S, s, G, 2)
        if nxt:
            gates_exp_act(act, S, s, G + 1)
        bias_act(act, S, s, G, 3)
        if nxt:
            gates_copy_act(act, S, s, G + 1, 1 - u)
        if nxt2:
            norm_std_act(act, S, s, G + 2, u)

    groups(act, body)


def ffn_dve(dve, S, s, ready):
    turn_lo_dve(dve, S, s, 0, 0)
    gates_dve(dve, S, s, 0, 0)

    def body(G, u, nxt, nxt2):
        experts_dve(dve, S, s, G, u, 0)
        if nxt:
            turn_lo_dve(dve, S, s, G + 1, 1 - u)
        experts_dve(dve, S, s, G, u, 1)
        experts_dve(dve, S, s, G, u, 2)
        if nxt:
            gates_dve(dve, S, s, G + 1, 1 - u)
        experts_dve(dve, S, s, G, u, 3)
        if nxt2:
            norm_stats_dve(dve, S, s, G + 2, u, lambda: ready(G + 2, u))
            norm_apply_dve(dve, S, s, G + 2, u)

    groups(dve, body)


def ffn_pool(pool, S, s, also):
    def body(G, u, nxt, nxt2):
        for t in range(GT):
            add_pool(pool, S, s, G, t)
            if nxt2:
                also(G + 2, u, t)
    groups(pool, body)


def store_groups(sp, S, s, dst, also):
    stored = (s.stored0, s.stored1)
    rows = dst.rearrange("(n p) d -> p n d", p=P)

    def body(G, u, nxt, nxt2):
        if nxt2:
            also(G + 2, u)
        sp.wait_ge(s.added, GT * (G + 1) + 2)
        if not (isinstance(G, int) and G < 2):
            sp.wait_ge(stored[u], 16 * (G // 2 if isinstance(G, int) else (G - u) // 2))
        sp.dma_start(rows[:, ds(G * GT, GT), :],
                     S.m.xs[:, ds(G * GT * D, GT * D)].rearrange("p (n d) -> p n d", d=D)).then_inc(stored[u], 16)
    groups(sp, body)
    for u in range(2):
        sp.wait_ge(stored[u], 16 * NG // 2)



def ffn1_dma(sp, S):
    m, ins, s = S.m, S.ins, S.f1
    x_rows = ins["x"].rearrange("(n p) d -> p n d", p=P)
    x_in = (s.x_in0, s.x_in1)

    def load_x(G, u):
        if not (isinstance(G, int) and G < 2):
            sp.wait_ge(x_in[u], 16 * (G // 2 if isinstance(G, int) else (G - u) // 2))
        sp.dma_start(m.xs[:, ds(G * GT * D, GT * D)].rearrange("p (n d) -> p n d", d=D),
                     x_rows[:, ds(G * GT, GT), :]).then_inc(x_in[u], 16)

    sp.dma_start(m.ident[:, :], ins["c_ident"]).then_inc(S.consts_in, 16)
    load_x(0, 0)
    load_x(1, 1)
    load_expert_weights(sp, S, s)
    for name, dst in (("c_ident16", m.ident16), ("c_tri", m.tri), ("c_mask_q", m.mask_q),
                      ("c_mask_k", m.mask_k), ("c_off", m.off), ("c_mparts", m.mparts)):
        sp.dma_start(dst[:, :], ins[name]).then_inc(S.consts_in, 16)
    store_groups(sp, S, s, S.x1_d, load_x)


CONST_LOADS = 16 * 7


def ffn1_pe(pe, S):
    s = S.f1
    pe.wait_ge(S.consts_in, CONST_LOADS)

    def free_tb(G):
        if not (isinstance(G, int) and G == 0):
            pe.wait_ge(s.lo, KD * G)
    ffn_pe(pe, S, s, None, free_tb, lambda G, u: None)


def ffn1_act(act, S):
    s = S.f1
    act.wait_ge(S.ones_set, 1)
    norm_std_act(act, S, s, 0, 0)
    norm_std_act(act, S, s, 1, 1)
    split_weights_act(act, S, s)
    ffn_act(act, S, s, lambda G, u: None)


def ffn1_dve(dve, S):
    s = S.f1
    x_in = (s.x_in0, s.x_in1)
    dve.memset(S.m.eps[:, :], EPS).then_inc(S.ones_set, 1)
    dve.memset(S.m.zero16[:, :], 0.0).then_inc(S.ones_set, 1)
    dve.sem_inc(s.used, E)

    def ready(G, u):
        wait_alone(dve, S, x_in[u], 16 * (G // 2 + 1 if isinstance(G, int) else (G - u) // 2 + 1))
    for G in range(2):
        norm_stats_dve(dve, S, s, G, G, lambda: ready(G, G))
        norm_apply_dve(dve, S, s, G, G)
    split_weights_dve(dve, S, s)
    dve.wait_ge(S.consts_in, CONST_LOADS)
    ffn_dve(dve, S, s, ready)


def ffn1_pool(pool, S):
    pool.sem_inc(S.f1.added, 2)
    ffn_pool(pool, S, S.f1, lambda G, u, t: None)



def project_dma(sp, S):
    m, ins, s = S.m, S.ins, S.pj
    for i, name in enumerate(("WqT", "WkT", "WvT")):
        sp.dma_start(m.qkv_raw[:, :].rearrange("p (w k e) -> p w k e", w=3, k=KD)[:, i],
                     ins[name].rearrange("(k p) e -> p k e", p=P)).then_inc(s.w_in, 16)
    for i, name in enumerate(("bq", "bk")):
        sp.dma_start(m.qk_bias[:, 2 * i:2 * i + 2], ins[name].rearrange("(k p) -> p k", p=P),
                     allow_slow_non_contiguous=True).then_inc(s.w_in, 16)
    sp.dma_start(m.v_bias[:, :], ins["bv"].rearrange("(a n) -> a n", a=1).broadcast_to([P, D])).then_inc(s.w_in, 16)
    parts_out = (s.parts_out0, s.parts_out1)
    v_out = (s.v_out0, s.v_out1)

    def body(G, u, nxt, nxt2):
        for i in range(4):
            sp.wait_ge(s.part3, 4 * G + i + 1)
            sp.dma_start(S.qk_d[i // 2, :, (i % 2) * P:(i % 2 + 1) * P, ds(G * GW, GW)].rearrange("c p t -> p c t"),
                         m.parts[i % 2][:, :].rearrange("p (c t) -> p c t", c=3)).then_inc(parts_out[i % 2], 16)
        sp.wait_ge(s.v_copied, 2 * (G + 1) + 2)
        for t in range(GT):
            sp.dma_start(S.v_d[:, ds(G * GT + t, 1), :, :].rearrange("g n p f -> p (g n) f"),
                         m.vpad[u][:, t * 512:(t + 1) * 512].rearrange("p (g f) -> p g f", g=NHG)).then_inc(v_out[u], 16)
    groups(sp, body)
    for i in range(2):
        sp.wait_ge(parts_out[i], 16 * 2 * NG)
        sp.wait_ge(v_out[i], 16 * GT * NG // 2)


PJ_LOADS = 16 * 6


def project_pe(pe, S):
    m, s = S.m, S.pj

    def free_tb(G):
        if not (isinstance(G, int) and G == 0):
            pe.wait_ge(s.lo, KD * G)
    pe.wait_ge(s.w_lo, 1)
    turn_pe(pe, S, s, 0, 0, lambda: free_tb(0))

    def body(G, u, nxt, nxt2):
        pe.wait_ge(s.lo, KD * (G + 1))
        for i in range(4):
            if i == 2 and nxt:
                turn_pe(pe, S, s, G + 1, 1 - u, lambda: free_tb(G + 1))
            pe.wait_ge(s.qk_copied, 4 * G + i + 1)
            w = (i // 2) * KD * D + (i % 2) * P
            split_product(pe, S.exb[i],
                          lambda k: m.qkv_hi[:, w + k * D:w + k * D + P], lambda k: m.qkv_lo[:, w + k * D:w + k * D + P],
                          lambda k: m.xt_hi[u][:, k * GW:(k + 1) * GW], lambda k: m.xt_lo[u][:, k * GW:(k + 1) * GW],
                          range(KD)).then_inc(s.qk, 1)
        w = 2 * KD * D
        for t in range(GT):
            bank = (S.gb, S.rb)[t // 2]
            if t % 2 == 0:
                pe.wait_ge(s.v_copied, 2 * G + t // 2 + 1)
            last = split_product(pe, bank[:, (t % 2) * D:(t % 2 + 1) * D],
                          lambda k: m.xt_hi[u][:, k * GW + t * P:k * GW + (t + 1) * P],
                          lambda k: m.xt_lo[u][:, k * GW + t * P:k * GW + (t + 1) * P],
                          lambda k: m.qkv_hi[:, w + k * D:w + (k + 1) * D], lambda k: m.qkv_lo[:, w + k * D:w + (k + 1) * D],
                          range(KD))
            if t % 2:
                last.then_inc(s.v, 1)
    groups(pe, body)


def project_act(act, S):
    m, s = S.m, S.pj
    parts_out = (s.parts_out0, s.parts_out1)
    norm_std_act(act, S, s, 0, 0)
    norm_std_act(act, S, s, 1, 1)
    act.wait_ge(s.w_in, PJ_LOADS)
    act.activation(m.qkv_hi[:, :], m.qkv_raw[:, :], ACT.Copy).then_inc(s.w_hi, 1)

    def free_xt(G):
        if not (isinstance(G, int) and G == 0):
            act.wait_ge(s.v, 2 * (G - 1))
    turn_hi_act(act, S, s, 0, 0, lambda: free_xt(0))

    def part2(G, i):
        act.wait_ge(s.split, 4 * G + i + 1)
        act.activation(m.parts[i % 2][:, GW:2 * GW], m.tr[i % 2][:, :], ACT.Copy).then_inc(s.part2, 1)

    def body(G, u, nxt, nxt2):
        for i in range(4):
            if i == 2 and nxt:
                turn_hi_act(act, S, s, G + 1, 1 - u, lambda: free_xt(G + 1))
            act.wait_ge(s.qk, 4 * G + i + 1)
            act.activation(m.tq[i % 2][:, :], S.exb[i][:, :], ACT.Identity, bias=m.qk_bias[:, i:i + 1],
                           scale=0.25 if i < 2 else 1.0).then_inc(s.qk_copied, 1)
            if not (isinstance(G, int) and G == 0 and i < 2):
                act.wait_ge(parts_out[i % 2], 16 * (2 * G + i // 2))
            act.wait_ge(s.qk_copied, 4 * G + i + 5)
            act.activation(m.parts[i % 2][:, 0:GW], m.tq[i % 2][:, :], ACT.Copy).then_inc(s.part1, 1)
            if i:
                part2(G, i - 1)
        part2(G, 3)
        if nxt2:
            norm_std_act(act, S, s, G + 2, u)
    groups(act, body)


def project_pool(pool, S):
    m, s = S.m, S.pj

    def body(G, u, nxt, nxt2):
        for i in range(4):
            pool.wait_ge(s.part1, 4 * G + i + 1)
            pool.tensor_tensor(m.tr[i % 2][:, :], m.tq[i % 2][:, :], m.parts[i % 2][:, 0:GW],
                               ALU.subtract).then_inc(s.split, 1)
    groups(pool, body)


def project_dve(dve, S):
    m, s = S.m, S.pj
    v_out = (s.v_out0, s.v_out1)
    dve.sem_inc(s.qk_copied, 4)
    dve.sem_inc(s.v_copied, 2)
    for u in range(2):
        dve.memset(m.vpad[u][:, :], 1.0).then_inc(S.ones_set, 1)
    for G in range(2):
        norm_stats_dve(dve, S, s, G, G, lambda: None)
        norm_apply_dve(dve, S, s, G, G)
    dve.wait_ge(s.w_hi, 1)
    dve.tensor_scalar(m.qk_bias[:, 0:2], m.qk_bias[:, 0:2], 0.25, None, ALU.mult)
    dve.tensor_tensor(m.qkv_lo[:, :], m.qkv_raw[:, :], m.qkv_hi[:, :].bitcast(fp32), ALU.subtract).then_inc(s.w_lo, 1)
    turn_lo_dve(dve, S, s, 0, 0)
    dve.wait_ge(S.ones_set, 4)

    def body(G, u, nxt, nxt2):
        for i in range(4):
            if i == 2 and nxt:
                turn_lo_dve(dve, S, s, G + 1, 1 - u)
            dve.wait_ge(s.part2, 4 * G + i + 1)
            dve.tensor_tensor(m.parts[i % 2][:, 2 * GW:3 * GW], m.tr[i % 2][:, :], m.parts[i % 2][:, GW:2 * GW],
                              ALU.subtract).then_inc(s.part3, 1)
        if not (isinstance(G, int) and G < 2):
            dve.wait_ge(v_out[u], 16 * GT * (G // 2 if isinstance(G, int) else (G - u) // 2))
        for h in range(2):
            dve.wait_ge(s.v, 2 * G + h + 1)
            bank = (S.gb, S.rb)[h]
            for t in range(2):
                ins = dve.tensor_tensor(
                    m.vpad[u][:, (2 * h + t) * 512:(2 * h + t + 1) * 512].rearrange("p (h d) -> p h d", h=H)[:, :, 0:HD],
                    bank[:, t * D:(t + 1) * D].rearrange("p (h d) -> p h d", h=H),
                    m.v_bias[:, :].rearrange("p (h d) -> p h d", h=H), ALU.add)
            ins.then_inc(s.v_copied, 1)
        if nxt2:
            norm_stats_dve(dve, S, s, G + 2, u, lambda: None)
            norm_apply_dve(dve, S, s, G + 2, u)
    groups(dve, body)



def index(qb, hg, kc):
    return 2 * qb * (qb + 1) + hg * (qb + 1) + kc


def q_blocks(eng, body):
    body(0)
    body(1)
    with eng.Fori(2, NQB - 1) as qb:
        body(qb)
    body(NQB - 1)


def chunks(eng, qb, body):
    if isinstance(qb, int) and qb == 0:
        body(0, True, True)
        return
    body(0, True, False)
    if not (isinstance(qb, int) and qb == 1):
        with eng.Fori(1, qb) as kc:
            body(kc, False, False)
    body(qb, False, True)


def maxima_of(qb, hg):
    if hg < 2:
        return qb, hg + 2
    if isinstance(qb, int) and qb == NQB - 1:
        return None
    return qb + 1, hg - 2


def step_after(qb, hg):
    if hg < NHG - 1:
        return qb, hg + 1
    if isinstance(qb, int) and qb == NQB - 1:
        return None
    return qb + 1, 0


def scores_pe(pe, S, qb, hg, kc, diag, idx):
    m, a = S.m, S.a
    half, j = idx // HG, idx % HG
    out = S.es[idx % 2]
    pe.wait_ge(a.exp, 8 * index(qb, hg, kc) + idx + 1)
    for b in range(2):
        c = 2 * half + b
        q0 = c * P if diag else 0
        last = pe.matmul(out[:, b * 512 + q0:(b + 1) * 512],
                         m.K[0:KR + AR + MR, ds((hg * HG + j) * L + kc * QB + c * P, P)],
                         m.Q[0:KR + AR + MR, (hg * HG + j) * QB + q0:(hg * HG + j + 1) * QB], start=True, stop=not diag)
        if diag:
            last = pe.matmul(out[:, b * 512 + q0:b * 512 + q0 + P], m.ident16[:, :], m.mask_k[:, :], start=False, stop=True)
    last.then_inc(a.st, 1)


FIRST_ORDER = ("S0 S1 M0 M1 P0 M2 M3 S2 M4 S3 M5 M6 P1 M7 M8 R S4 S5 M9 M10 P2 "
               "M11 M12 S6 S7 M13 M14 P3 M15").split()
ORDER = ("S0 S1 M0 M1 M2 P0 M3 S2 M4 S3 M5 M6 P1 M7 M8 S4 S5 M9 M10 P2 "
         "M11 M12 S6 M13 S7 M14 P3 M15").split()


def maxima_tiles(mx, hg, kc, diag):
    if diag and hg >= 2:
        return [t for i in range(16) for t in ((i, kc, False), (i, mx[0], True))]
    return [(i, kc, diag) for i in range(16)]


def maxima_bank(r, tiles, wide):
    return r % 2 if not wide else 1 if (r, tiles) == (15, 16) else r % 3


def maxima_pe(pe, S, mx, kc0, r, tiles, wide):
    m, a = S.m, S.a
    qb, hg = mx
    i, kc, diag = tiles[r]
    j, qs = i // 4, i % 4
    h = hg * HG + j
    w = (qs + 1) * P if diag else QB
    still_open = 2 if wide and r >= 2 and (r, len(tiles)) != (15, 16) else 1
    pe.wait_ge(a.mx, 16 * index(qb, hg, kc0) + r - still_open + 3)
    bank = S.mb[maxima_bank(r, len(tiles), wide)]
    last = pe.matmul(bank[:, 0:w], m.Q[0:KR + AR, h * QB + qs * P:h * QB + (qs + 1) * P],
                     m.K[0:KR + AR, ds(h * L + kc * QB, w)], start=True, stop=not diag)
    if diag:
        last = pe.matmul(bank[:, w - P:w], m.ident16[:, :], m.mask_q[:, :], start=False, stop=True)
    last.then_inc(a.m, 1)


def maxima_begin_pe(pe, S, qb, hg):
    pe.wait_ge(S.a.q_in[hg], 16 * 6 * (qb + 1))
    if hg == 0:
        pe.wait_ge(S.a.k_in, 16 * 6 * (qb + 1))


def values_pe(pe, S, half, b, diag, last_inc):
    m = S.m
    c = 2 * half + b
    q0 = c * P if diag else 0
    for j in range(HG):
        last = pe.matmul(S.ob[32 * j:32 * j + 32, q0:512], m.V[half][:, b * P + 32 * j:b * P + 32 * j + 32],
                         m.prob[half][:, (2 * j + b) * QB + q0:(2 * j + b + 1) * QB], start=False, stop=True,
                         skip_group_check=True)
    if last_inc:
        last.then_inc(S.a.pv, 1)


def shift_rows_pe(pe, S, s_next, hg):
    m, a = S.m, S.a
    pe.wait_ge(a.mp, s_next + 1)
    for j in range(HG):
        for qs in range(4):
            c = ((hg * HG + j) * 4 + qs) * (AR + MR)
            last = pe.matmul(S.xb[32 * j:32 * j + AR + MR, qs * P:(qs + 1) * P], m.mparts[:, c:c + AR + MR],
                             m.ident16[:, :], start=True, stop=True)
    last.then_inc(a.mt, 1)


def attend_pe(pe, S):
    m, a = S.m, S.a
    pe.sem_inc(a.exp, 2)
    pe.sem_inc(a.mx, 3)
    pe.sem_inc(a.pv, 1)
    pe.wait_ge(a.rows_in, 16 * (H + 1))
    for hg in range(2):
        maxima_begin_pe(pe, S, 0, hg)
        for i in range(16):
            maxima_pe(pe, S, (0, hg), 0, i, maxima_tiles((0, hg), 0, 0, True), False)
    shift_rows_pe(pe, S, 0, 0)

    def step(qb, hg):
        s = NHG * qb + hg
        is_first = isinstance(s, int) and s == 0
        mx = maxima_of(qb, hg)
        nxt = step_after(qb, hg)
        if mx:
            maxima_begin_pe(pe, S, *mx)
        else:
            pe.wait_ge(a.mx, 16 * index(NQB, 0, 0) + 3)
        pe.wait_ge(a.qrow, HG * (s + 1))

        def chunk(kc, first, diag):
            n = index(qb, hg, kc)
            for part in FIRST_ORDER if first else ORDER:
                what, i = part[0], int(part[1:] or 0)
                if what == "S":
                    scores_pe(pe, S, qb, hg, kc, diag, i)
                elif what == "M":
                    if mx:
                        tiles = maxima_tiles(mx, hg, kc, diag)
                        each = len(tiles) // 16
                        for r in range(each * i, each * i + each):
                            if r == 2 and not first and nxt:
                                pe.wait_ge(a.qrow, HG * (s + 2))
                            maxima_pe(pe, S, mx, kc, r, tiles, not first)
                elif what == "R":
                    if nxt:
                        shift_rows_pe(pe, S, s + 1, nxt[1])
                elif i < 2:
                    if not (is_first and first):
                        if i == 0:
                            pe.wait_ge(a.exp, 8 * n + 2)
                            pe.wait_ge(a.v_in[1], 16 * n)
                        values_pe(pe, S, 1, i, first, i == 1)
                else:
                    if i == 2:
                        if first:
                            if not is_first:
                                pe.wait_ge(a.o_copied, s)
                            pe.matmul(S.ob[:, :], m.zero16[:, 0:P], m.zero16[:, :], start=True, stop=True)
                        pe.wait_ge(a.exp, 8 * n + 4 + 2)
                        pe.wait_ge(a.v_in[0], 16 * (n + 1))
                    values_pe(pe, S, 0, i - 2, diag, i == 3)

        chunks(pe, qb, chunk)

    q_blocks(pe, lambda qb: [step(qb, hg) for hg in range(NHG)])
    n = index(NQB - 1, NHG - 1, NQB)
    pe.wait_ge(a.exp, 8 * n + 2)
    pe.wait_ge(a.v_in[1], 16 * n)
    for b in range(2):
        values_pe(pe, S, 1, b, True, b == 1)


def shift_row_act(act, S, s_next, hg, j):
    m, a = S.m, S.a
    h = hg * HG + j
    if j == 0:
        act.wait_ge(a.mt, s_next + 1)
    act.activation(m.Q[KR:KR + AR + MR, h * QB:(h + 1) * QB], S.xb[32 * j:32 * j + AR + MR, :],
                   ACT.Copy).then_inc(a.qrow, 1)


def attend_act(act, S):
    m, a = S.m, S.a

    def copy_out(n, par, stored):
        act.wait_ge(a.pv, 2 * n + 1)
        if not (isinstance(stored, int) and stored == 0):
            act.wait_ge(a.at_out[par], 16 * stored)
        act.activation(m.o[par][:, :], S.ob[:, :], ACT.Copy).then_inc(a.o_copied, 1)

    for j in range(HG):
        shift_row_act(act, S, 0, 0, j)

    def step(qb, hg):
        s = NHG * qb + hg
        nxt = step_after(qb, hg)

        def chunk(kc, first, diag):
            n = index(qb, hg, kc)
            for idx in range(8):
                half, j = idx // HG, idx % HG
                if idx % HG == 0:
                    act.wait_ge(a.pv, 2 * n + half)
                wait_alone(act, S, a.st, 8 * n + idx + 1)
                at = (hg * HG + j) * CW + (NQB - 1)
                bias = m.off[:, at:at + 1] if diag else m.off[:, ds(at - qb + kc, 1)]
                base = 2 * j * QB
                if diag:
                    for b in range(2):
                        q0 = (2 * half + b) * P
                        last = act.activation(m.prob[half][:, base + b * QB + q0:base + (b + 1) * QB],
                                              S.es[idx % 2][:, b * 512 + q0:(b + 1) * 512], ACT.Exp, bias=bias)
                else:
                    last = act.activation(m.prob[half][:, base:base + 2 * QB], S.es[idx % 2][:, :], ACT.Exp, bias=bias)
                last.then_inc(a.exp, 1)
                if first and nxt and idx >= 4:
                    shift_row_act(act, S, s + 1, nxt[1], idx - 4)
                if first and idx == 4 and not (isinstance(s, int) and s == 0):
                    copy_out(n, (hg - 1) % 2, 2 * qb + (hg - 1) // 2)
        chunks(act, qb, chunk)

    q_blocks(act, lambda qb: [step(qb, hg) for hg in range(NHG)])
    copy_out(index(NQB - 1, NHG - 1, NQB), 1, 2 * NQB - 1)


def attend_dve(dve, S):
    m, a = S.m, S.a
    for buf in m.pm:
        dve.memset(buf[:, :], -1.0e38).then_inc(a.pm_set, 1)
    dve.wait_ge(a.pm_set, 2)
    pm = [buf[:, :].rearrange("p (j c) -> p j c", c=NQB) for buf in m.pm]
    pmo = [buf[:, :].rearrange("p (j c) -> p j c", c=NQB + 1) for buf in m.pmo]

    def finish(qb, hg):
        s = NHG * qb + hg
        own = 3 * s
        off = m.off[:, :].rearrange("p (h c) -> p h c", h=H)[:, hg * HG:(hg + 1) * HG, ds(NQB - 1 - qb, NQB)]
        parts = m.mparts[:, hg * 16 * 8:(hg + 1) * 16 * 8].rearrange("p (j c) -> p j c", c=AR + MR)

        def offsets():
            wait_alone(dve, S, a.mx, 16 * (index(qb, hg, qb) + 1) + 3)
            for j in range(HG):
                ins = dve.tensor_tensor(pmo[hg % 2][:, 4 * j:4 * j + 4, 0:NQB], pm[hg % 2][:, 4 * j:4 * j + 4, :],
                                        off[:, j:j + 1, :].broadcast_to([P, 4, NQB]), ALU.add)
            ins.then_inc(a.fin, 1)

        def maximum():
            dve.wait_ge(a.fin, own + 1)
            dve.tensor_reduce(m.nmax[:, :], pmo[hg % 2], axis=AX.X, op=ALU.max, negate=True).then_inc(a.fin, 1)

        def high():
            dve.wait_ge(a.fin, own + 2)
            dve.tensor_copy(parts[:, :, AR], m.nmax[:, :]).then_inc(a.fin, 1)

        def low():
            dve.wait_ge(a.fin, own + 3)
            dve.tensor_tensor(parts[:, :, AR + 1], m.nmax[:, :], parts[:, :, AR], ALU.subtract).then_inc(a.mp, 1)
        return [offsets, maximum, high, low]

    def reduce(mx, kc0, tiles, wide, between):
        n = index(mx[0], mx[1], kc0)
        for r, (i, kc, diag) in enumerate(tiles):
            w = (i % 4 + 1) * P if diag else QB
            wait_alone(dve, S, a.m, 16 * n + r + 1)
            to = pmo[mx[1] % 2][:, i, NQB:NQB + 1] if diag else m.pm[mx[1] % 2][:, ds(i * NQB + kc, 1)]
            dve.tensor_reduce(to, S.mb[maxima_bank(r, len(tiles), wide)][:, 0:w], axis=AX.X, op=ALU.max).then_inc(a.mx, 1)
            if 1 <= r <= len(between):
                between[r - 1]()

    def reciprocals(s):
        dve.wait_ge(a.sums_in, 16 * s)
        if not (isinstance(s, int) and s == 1):
            dve.wait_ge(a.recips_out, 16 * (s - 1))
        dve.reciprocal(m.recips[:, :], m.sums[:, :]).then_inc(a.recip, 1)

    for hg in range(2):
        reduce((0, hg), 0, maxima_tiles((0, hg), 0, 0, True), False, finish(0, 0) if hg else [])

    def step(qb, hg):
        s = NHG * qb + hg
        mx = maxima_of(qb, hg)
        ended = step_after(qb, hg)

        def chunk(kc, first, diag):
            between = finish(*ended) if first and ended else []
            if mx:
                reduce(mx, kc, maxima_tiles(mx, hg, kc, diag), not first, between)
            elif first:
                for part in between:
                    part()
        chunks(dve, qb, chunk)
        if not (isinstance(s, int) and s == 0):
            reciprocals(s)

    q_blocks(dve, lambda qb: [step(qb, hg) for hg in range(NHG)])
    reciprocals(NHG * NQB)


def load_queries(sp, S, qb, hg):
    for c, part in enumerate(Q_PART):
        sp.dma_start(S.m.Q[HD * c:HD * (c + 1), hg * HG * QB:(hg + 1) * HG * QB].rearrange("d (j t) -> d j t", j=HG),
                     S.qk_d[0, part, hg * HG * HD:(hg + 1) * HG * HD, ds(qb * QB, QB)].rearrange("(j d) t -> d j t", d=HD)
                     ).then_inc(S.a.q_in[hg], 16)


def attend_dma(sp, S):
    m, a, ins = S.m, S.a, S.ins
    for h in range(H):
        sp.dma_start(m.K[KR:KR + AR + MR, h * L:(h + 1) * L], ins["c_krows"]).then_inc(a.rows_in, 16)
    sp.dma_start(m.Q[KR:KR + AR + MR, :], ins["c_qrows"]).then_inc(a.rows_in, 16)
    for hg in range(NHG):
        load_queries(sp, S, 0, hg)

    def step(qb, hg):
        first = index(qb, hg, 0)
        if hg:
            if not (isinstance(qb, int) and qb == NQB - 1):
                sp.wait_ge(a.st, 8 * first)
                load_queries(sp, S, qb + 1, hg - 1)
        elif not (isinstance(qb, int) and qb == 0):
            sp.wait_ge(a.st, 8 * first)
            load_queries(sp, S, qb, NHG - 1)

        def chunk(kc, first, diag):
            n = index(qb, hg, kc)
            for half in range(2):
                sp.wait_ge(a.pv, 2 * n + half)
                sp.dma_start(m.V[half][:, :].rearrange("p (k f) -> p k f", k=2),
                             S.v_d[hg, ds(kc * 4 + 2 * half, 2), :, :].rearrange("k p f -> p k f")).then_inc(a.v_in[half], 16)
        chunks(sp, qb, chunk)

    q_blocks(sp, lambda qb: [step(qb, hg) for hg in range(NHG)])


def attend_pool(pool, S):
    m, a = S.m, S.a

    def load_keys(kc):
        if not (isinstance(kc, int) and kc == 0):
            pool.wait_ge(a.k_in, 16 * 6 * kc)
        for c, part in enumerate(K_PART):
            pool.dma_start(m.K[HD * c:HD * (c + 1), :].rearrange("d (h t) -> d h t", h=H)[:, :, ds(kc * QB, QB)],
                           S.qk_d[1, part, :, ds(kc * QB, QB)].rearrange("(h d) t -> d h t", d=HD)).then_inc(a.k_in, 16)

    def store(qb, hg, s):
        o = m.o[hg % 2]
        wait_alone(pool, S, a.o_copied, s)
        for j in range(HG):
            pool.dma_start(S.sums_d[j:j + 1, :], o[32 * j + HD:32 * j + HD + 1, :]).then_inc(a.sums_out, 16)
        wait_alone(pool, S, a.sums_out, 16 * HG * s)
        pool.dma_start(m.sums[:, :], S.sums_d.rearrange("j (b c) -> (j b) c", c=HG * QB // P)).then_inc(a.sums_in, 16)
        wait_alone(pool, S, a.recip, s)
        pool.dma_start(S.recips_d.rearrange("j (b c) -> (j b) c", c=HG * QB // P), m.recips[:, :]).then_inc(a.recips_out, 16)
        wait_alone(pool, S, a.recips_out, 16 * s)
        if not (isinstance(s, int) and s == 1):
            wait_alone(pool, S, a.normed, s - 1)
        for j in range(HG):
            pool.dma_start(m.rden[32 * j:32 * j + 32, :], S.recips_d[j:j + 1, :].broadcast_to([32, QB])).then_inc(a.recips_in, 16)
        wait_alone(pool, S, a.recips_in, 16 * HG * s)
        pool.tensor_tensor(o[:, :], o[:, :], m.rden[:, :], ALU.mult).then_inc(a.normed, 1)
        pool.wait_ge(a.normed, s)
        pool.dma_start(S.at_d[hg, :, ds(qb * QB, QB)], o[:, :]).then_inc(a.at_out[hg % 2], 16)

    load_keys(0)

    def block(qb):
        last = isinstance(qb, int) and qb == NQB - 1
        if not last:
            load_keys(qb + 1)
        if not (isinstance(qb, int) and qb == 0):
            store(qb - 1, NHG - 1, NHG * qb)
        for hg in range(1, NHG):
            store(qb, hg - 1, NHG * qb + hg)
    q_blocks(pool, block)
    store(NQB - 1, NHG - 1, NHG * NQB)
    for par in range(2):
        pool.wait_ge(a.at_out[par], 16 * NHG * NQB // 2)



def ffn2_dma(sp, S):
    m, ins, s = S.m, S.ins, S.f2
    x_in = (s.x_in0, s.x_in1)
    at_in = (s.at_in0, s.at_in1)
    x_rows = S.x1_d.rearrange("(n p) d -> p n d", p=P)

    def load(G, u):
        n = G // 2 if isinstance(G, int) else (G - u) // 2
        if not (isinstance(G, int) and G < 2):
            sp.wait_ge(x_in[u], 16 * n)
            sp.wait_ge(at_in[u], 16 * n)
            sp.wait_ge(s.at_lo, NHG * (G - 1))
        sp.dma_start(m.at_raw[u][:, :].rearrange("p (g t) -> p g t", g=NHG),
                     S.at_d[:, :, ds(G * GW, GW)].rearrange("g p t -> p g t")).then_inc(at_in[u], 16)
        sp.dma_start(m.xs[:, ds(G * GT * D, GT * D)].rearrange("p (n d) -> p n d", d=D),
                     x_rows[:, ds(G * GT, GT), :]).then_inc(x_in[u], 16)

    load(0, 0)
    load(1, 1)
    sp.wait_ge(s.wo_set, 1)
    wo = ins["WoT"].rearrange("(g j d) e -> j d g e", g=NHG, j=HG)
    for j in range(HG):
        sp.dma_start(m.wo_raw[32 * j:32 * j + HD, :].rearrange("p (g e) -> p g e", g=NHG), wo[j]).then_inc(s.wo_in, 16)
    sp.dma_start(m.wo_raw[HD:HD + 1, 0:D], ins["bo"].rearrange("(a n) -> a n", a=1)).then_inc(s.wo_in, 16)
    load_expert_weights(sp, S, s)
    store_groups(sp, S, s, S.out, load)


WO_LOADS = 16 * (HG + 1)


def ffn2_pe(pe, S):
    m, s = S.m, S.f2

    def attended(G, u):
        pe.wait_ge(s.at_lo, NHG * (G + 1))
        if not (isinstance(G, int) and G < 2):
            pe.wait_ge(s.lo, KD * G)
        if not (isinstance(G, int) and G == 0):
            pe.wait_ge(s.x2, G)
        for t in range(GT):
            last = split_product(pe, S.tb[t // 2][:, (t % 2) * D:(t % 2 + 1) * D],
                                 lambda g: m.at_hi[:, g * GW + t * P:g * GW + (t + 1) * P],
                                 lambda g: m.at_lo[:, g * GW + t * P:g * GW + (t + 1) * P],
                                 lambda g: m.wo_hi[:, g * D:(g + 1) * D], lambda g: m.wo_lo[:, g * D:(g + 1) * D], range(NHG))
        last.then_inc(s.attended, 1)

    pe.wait_ge(s.wo_lo, 1)
    attended(0, 0)
    attended(1, 1)

    def free_tb(G):
        pe.wait_ge(s.x2, 2 if isinstance(G, int) and G == 0 else G + 1)
    ffn_pe(pe, S, s, None, free_tb, attended)


def ffn2_act(act, S):
    m, s = S.m, S.f2
    at_in = (s.at_in0, s.at_in1)

    def at_hi(G, u):
        n = G // 2 if isinstance(G, int) else (G - u) // 2
        act.wait_ge(at_in[u], 16 * (n + 1))
        if not (isinstance(G, int) and G == 0):
            act.wait_ge(s.attended, G)
        act.activation(m.at_hi[:, :], m.at_raw[u][:, :], ACT.Copy).then_inc(s.at_hi, 1)
    act.wait_ge(s.wo_in, WO_LOADS)
    act.activation(m.wo_hi[:, :], m.wo_raw[:, :], ACT.Copy).then_inc(s.wo_hi, 1)
    for G in range(2):
        at_hi(G, G)
        norm_std_act(act, S, s, G, G)
    split_weights_act(act, S, s)
    ffn_act(act, S, s, at_hi)


def ffn2_dve(dve, S):
    m, s = S.m, S.f2
    x_in = (s.x_in0, s.x_in1)
    dve.sem_inc(s.used, E)
    dve.memset(m.wo_raw[:, :], 0.0).then_inc(s.wo_set, 1)
    dve.wait_ge(s.wo_hi, 1)
    dve.tensor_tensor(m.wo_lo[:, :], m.wo_raw[:, :], m.wo_hi[:, :].bitcast(fp32), ALU.subtract).then_inc(s.wo_lo, 1)

    def ready(G, u):
        n = G // 2 if isinstance(G, int) else (G - u) // 2
        dve.wait_ge(x_in[u], 16 * (n + 1))
        dve.wait_ge(s.attended, G + 1)
        for k in range(2):
            x = m.xs[:, ds((G * GT + 2 * k) * D, 2 * D)]
            ins = dve.tensor_tensor(x, x, S.tb[k][:, :], ALU.add)
        ins.then_inc(s.x2, 1)
        wait_alone(dve, S, s.x2, G + 1)
    for G in range(2):
        norm_stats_dve(dve, S, s, G, G, lambda: ready(G, G))
        norm_apply_dve(dve, S, s, G, G)
    split_weights_dve(dve, S, s)
    ffn_dve(dve, S, s, ready)


def ffn2_pool(pool, S):
    m, s = S.m, S.f2
    pool.sem_inc(s.added, 2)

    def at_lo(G, u, g):
        c = slice(g * GW, (g + 1) * GW)
        if g == 0:
            pool.wait_ge(s.at_hi, G + 1)
        pool.tensor_tensor(m.at_lo[:, c], m.at_raw[u][:, c], m.at_hi[:, c].bitcast(fp32), ALU.subtract).then_inc(s.at_lo, 1)
    for G in range(2):
        for g in range(NHG):
            at_lo(G, G, g)
    ffn_pool(pool, S, s, at_lo)



def kernel(**inputs):
    import concourse.bacc as bacc
    from concourse.bass_utils import run_bass_kernel_spmd as run

    def arr(name):
        return np.ascontiguousarray(inputs[name])

    arrays = {
        "x": arr("L0_attn_x").reshape(L, D),
        "WqT": np.ascontiguousarray(arr("L0_attn_Wq").T), "bq": arr("L0_attn_bq"),
        "WkT": np.ascontiguousarray(arr("L0_attn_Wk").T), "bk": arr("L0_attn_bk"),
        "WvT": np.ascontiguousarray(arr("L0_attn_Wv").T), "bv": arr("L0_attn_bv"),
        "WoT": np.ascontiguousarray(arr("L0_attn_Wo").T), "bo": arr("L0_attn_bo"),
        "gate_wT": np.ascontiguousarray(arr("L0_ffn_gate_w").T), "gate_b": arr("L0_ffn_gate_b"),
        "expert_w": arr("L0_ffn_expert_w"), "expert_b": arr("L0_ffn_expert_b"),
    }
    arrays.update(constant_arrays())
    nc = bacc.Bacc("TRN2", target_bir_lowering=False, num_devices=1)
    ins = {n: nc.dram_tensor(n, v.shape, mybir.dt.from_np(v.dtype), kind="ExternalInput").ap() for n, v in arrays.items()}
    ins = {n: v.bitcast(bf16) if arrays[n].dtype == np.uint16 else v for n, v in ins.items()}
    out = nc.dram_tensor("out", [L, D], fp32, kind="ExternalOutput").ap()
    program(nc, ins, out)
    r = run(nc, [arrays], core_ids=[0])
    return r.results[0]["out"].reshape(1, L, D)
```

```python
from contextlib import ExitStack

import numpy as np
import concourse.bass as bass
from concourse import mybir

fp32 = mybir.dt.float32
f32r = mybir.dt.float32r
bf16 = mybir.dt.bfloat16
ALU = mybir.AluOpType
ACT = mybir.ActivationFunctionType
AX = mybir.AxisListType
ds = bass.ds


class Named:
    pass


L, D = 4096, 256
H, HD = 16, 16
E = 8
P = 128
KD = D // P
GT = 4
GW = GT * P
NG = L // GW
EPB = 512 // D
NB = E // EPB
EPS = 1e-5

QB = 512
NQB = L // QB
HG = 4
NHG = H // HG
KR = 96
AR = 6
MR = 2
Q_PART = (0, 1, 0, 1, 2, 0)
K_PART = (0, 0, 1, 1, 0, 2)
NEG = -1.0e30
CW = 2 * NQB - 1


def constant_arrays():
    def cut(v):
        return (np.ascontiguousarray(v, np.float32).view(np.uint32) & 0xFFFF0000).view(np.float32)

    def half(v):
        bits = np.ascontiguousarray(v, np.float32).view(np.uint32)
        assert not (bits & 0xFFFF).any()
        return (bits >> 16).astype(np.uint16)

    slope = np.power(np.float32(2.0), (-8.0 * np.arange(1, H + 1, dtype=np.float32) / H)).astype(np.float32)
    s1 = cut(slope)
    s2 = cut(slope - s1)
    s3 = cut(slope - s1 - s2)
    parts = np.stack([s1, s2, s3, s1, s2, s3])
    k = np.arange(L)
    k_rows = np.ones((AR + MR, L), np.float32)
    k_rows[0:3] = k % 256
    k_rows[3:6] = 256 * ((k // 256) % 2)
    q_rows = np.zeros((AR + MR, H, QB), np.float32)
    q_rows[0:AR] = parts[:, :, None]
    m_parts = np.zeros((NHG, HG, 4, AR + MR), np.float32)
    m_parts[..., 0:AR] = parts.T.reshape(NHG, HG, 1, AR)
    m_parts = np.broadcast_to(m_parts.reshape(1, -1), (P, NHG * 16 * 8))
    off = slope[:, None] * (np.float32(QB) * (np.arange(CW, dtype=np.float32) - (NQB - 1)))[None, :]
    p = np.arange(P)
    tri = (p[None, :E] < p[:E, None]).astype(np.float32)
    return {
        "c_ident": np.eye(P, dtype=np.float32),
        "c_ident16": half(np.eye(P)),
        "c_tri": np.broadcast_to(tri.reshape(1, E * E), (P, E * E)).copy(),
        "c_mask_q": half(cut(np.where(p[None, :] <= p[:, None], 0.0, NEG))),
        "c_mask_k": half(cut(np.where(p[None, :] >= p[:, None], 0.0, NEG))),
        "c_off": np.broadcast_to(off.reshape(1, H * CW), (P, H * CW)).astype(np.float32).copy(),
        "c_mparts": half(m_parts),
        "c_krows": half(k_rows),
        "c_qrows": half(q_rows.reshape(AR + MR, H * QB)),
    }


def plan_memory(nc):
    m = Named()
    at = [(nc.sbuf_base + 31) // 32 * 32]

    def put(name, cols, dt, parts=P):
        size = cols * (2 if dt == bf16 else 4)
        t = nc.alloc_sbuf_tensor_at(name, [parts, cols], dt, offset=at[0])
        at[0] += (size + 31) // 32 * 32
        return t

    m.ident = put("ident", P, fp32)
    m.ident16 = put("ident16", P, bf16)
    m.tri = put("tri", E * E, fp32)
    m.mask_q = put("mask_q", P, bf16)
    m.mask_k = put("mask_k", P, bf16)
    m.off = put("off", H * CW, fp32)
    m.mparts = put("mparts", NHG * 16 * 8, bf16)
    m.zero16 = put("zero16", 512, bf16)
    m.eps = put("eps", 1, fp32)

    m.pm = [put(f"pm{i}", 16 * NQB, fp32) for i in range(2)]
    m.pmo = [put(f"pmo{i}", 16 * (NQB + 1), fp32) for i in range(2)]
    m.nmax = put("nmax", 16, fp32)
    m.Q = put("Q", H * QB, bf16)
    keys = at[0]
    m.w_raw = put("w_raw", KD * E * D, fp32)
    m.w_hi = put("w_hi", KD * E * D, f32r)
    m.w_lo = put("w_lo", KD * E * D, f32r)
    m.xs = put("xs", NG * GT * D, fp32)
    slot = at[0]
    m.vpad = [put(f"vpad{u}", GT * H * 32, fp32) for u in range(2)]
    at[0] = slot
    m.at_raw = [put(f"at_raw{u}", NHG * GW, fp32) for u in range(2)]
    m.g_raw = put("g_raw", KD * E, fp32)
    m.gb = put("gb", 1, fp32)
    m.eb = put("eb", D, fp32)
    m.g_hi = put("g_hi", KD * E, f32r)
    m.g_lo = put("g_lo", KD * E, f32r)
    assert at[0] - keys <= 7 * H * QB * 2
    m.xh = [put(f"xh{u}", GT * D, fp32) for u in range(2)]
    m.xt_hi = [put(f"xt_hi{u}", KD * GW, f32r) for u in range(2)]
    m.xt_lo = [put(f"xt_lo{u}", KD * GW, f32r) for u in range(2)]
    m.bst = put("bst", GT * 6, fp32)
    m.mv = [put(f"mv{u}", GT * 2, fp32) for u in range(2)]
    m.std = put("std", GT, fp32)
    m.rstd = put("rstd", GT, fp32)
    m.lgt = put("lgt", GW, fp32)
    m.lg = put("lg", GT * E, fp32)
    m.top = put("top", GT, fp32)
    m.dl = put("dl", GT * E, fp32)
    m.ex = put("ex", GT * E, fp32)
    m.gtr = put("gtr", GT * E * E, fp32)
    m.eqr = put("eqr", GT * E * E, fp32)
    m.rank = put("rank", GT * E, fp32)
    m.gsum = put("gsum", GT, fp32)
    m.grec = put("grec", GT, fp32)
    m.gates = [put(f"gates{u}", GT * E, fp32) for u in range(2)]
    m.gts = [put(f"gts{u}", GW, fp32) for u in range(2)]
    m.acc = [put(f"acc{i}", D, fp32) for i in range(2)]
    after_ffn = at[0]
    m.qkv_raw = put("qkv_raw", KD * 3 * D, fp32)
    m.qkv_hi = put("qkv_hi", KD * 3 * D, f32r)
    m.qkv_lo = put("qkv_lo", KD * 3 * D, f32r)
    m.qk_bias = put("qk_bias", 4, fp32)
    m.v_bias = put("v_bias", D, fp32)
    m.tq = [put(f"tq{i}", GW, fp32) for i in range(4)]
    m.tr = [put(f"tr{i}", GW, fp32) for i in range(4)]
    m.parts = [put(f"parts{i}", 3 * GW, bf16) for i in range(4)]
    end_a = at[0]
    at[0] = after_ffn
    m.at_hi = put("at_hi", NHG * GW, f32r)
    m.at_lo = put("at_lo", NHG * GW, f32r)
    end_c = at[0]
    at[0] = keys
    m.K = put("K", H * L, bf16)
    m.prob = [put(f"prob{p}", HG * 2 * QB, fp32) for p in range(2)]
    end_prob = at[0]
    assert end_c <= end_prob
    m.V = [put(f"V{p}", 2 * P, fp32) for p in range(2)]
    m.o = [put(f"o{i}", QB, fp32) for i in range(2)]
    m.rden = put("rden", QB, fp32)
    m.sums = put("sums", HG * QB // P, fp32)
    m.recips = put("recips", HG * QB // P, fp32)
    m.wo_raw = put("wo_raw", NHG * D, fp32)
    m.wo_hi = put("wo_hi", NHG * D, f32r)
    m.wo_lo = put("wo_lo", NHG * D, f32r)
    end_b = at[0]
    assert max(end_a, end_b, end_c) <= nc.sbuf_usable_end, (end_a, end_b, end_c)
    return m


def program(nc, ins, out):
    ctx = ExitStack()
    with ctx:
        m = plan_memory(nc)
        bank = [ctx.enter_context(nc.psum_tensor(f"bank{i}", [P, 512], fp32)) for i in range(4)]
        pair = [ctx.enter_context(nc.psum_tensor(f"pair{i}", [P, 1024], fp32)) for i in range(2)]
        exb = [pair[0][:, 0:512], pair[0][:, 512:1024], pair[1][:, 0:512], pair[1][:, 512:1024]]
        tb = [bank[0], bank[1]]
        gb = bank[2]
        rb = bank[3]
        mb = [bank[0], bank[1], bank[3]]
        ob = bank[2]
        xb = bank[3]

        def scratch(name, shape, dt):
            return nc.dram_tensor(name, shape, dt, kind="Internal").ap()

        x1_d = scratch("x1_d", [L, D], fp32)
        qk_d = scratch("qk_d", [2, 3, D, L], bf16)
        v_d = scratch("v_d", [NHG, L // P, P, P], fp32)
        at_d = scratch("at_d", [NHG, P, L], fp32)
        sums_d = scratch("sums_d", [HG, QB], fp32)
        recips_d = scratch("recips_d", [HG, QB], fp32)

        def sem(name):
            return ctx.enter_context(nc.semaphore(name))

        consts_in = sem("consts_in")
        ident_in = sem("ident_in")
        ones_set = sem("ones_set")
        phase_end = sem("phase_end")

        def norm_sems(k):
            s = Named()
            s.stats = sem(f"{k}_stats")
            s.std = sem(f"{k}_std")
            s.rstd = sem(f"{k}_rstd")
            s.xhat = sem(f"{k}_xhat")
            s.turned = sem(f"{k}_turned")
            s.hi = sem(f"{k}_hi")
            s.lo = sem(f"{k}_lo")
            return s

        def ffn_sems(k):
            s = norm_sems(k)
            s.w_in = sem(f"{k}_w_in")
            s.m_in = [sem(f"{k}_m_in{n}") for n in range(NB)]
            s.m_hi = sem(f"{k}_m_hi")
            s.m_lo = sem(f"{k}_m_lo")
            s.w_hi = sem(f"{k}_w_hi")
            s.w_lo = sem(f"{k}_w_lo")
            s.lgt = sem(f"{k}_lgt")
            s.lgt_copied = sem(f"{k}_lgt_copied")
            s.lg = sem(f"{k}_lg")
            s.soft = sem(f"{k}_soft")
            s.shifted = sem(f"{k}_shifted")
            s.ex = sem(f"{k}_ex")
            s.gates = sem(f"{k}_gates")
            s.gt = sem(f"{k}_gt")
            s.gt_copied = sem(f"{k}_gt_copied")
            s.bias = sem(f"{k}_bias")
            s.acc_set = sem(f"{k}_acc_set")
            s.experts = sem(f"{k}_experts")
            s.used = sem(f"{k}_used")
            s.added = sem(f"{k}_added")
            s.stored0 = sem(f"{k}_stored0")
            s.stored1 = sem(f"{k}_stored1")
            s.x_in0 = sem(f"{k}_x_in0")
            s.x_in1 = sem(f"{k}_x_in1")
            return s

        f1 = ffn_sems("f1")
        f2 = ffn_sems("f2")
        f2.wo_in = sem("f2_wo_in")
        f2.wo_hi = sem("f2_wo_hi")
        f2.wo_lo = sem("f2_wo_lo")
        f2.wo_set = sem("f2_wo_set")
        f2.at_in0 = sem("f2_at_in0")
        f2.at_in1 = sem("f2_at_in1")
        f2.at_hi = sem("f2_at_hi")
        f2.at_lo = sem("f2_at_lo")
        f2.attended = sem("f2_attended")
        f2.x2 = sem("f2_x2")
        pj = norm_sems("pj")
        pj.w_in = sem("pj_w_in")
        pj.w_hi = sem("pj_w_hi")
        pj.w_lo = sem("pj_w_lo")
        pj.qk = sem("pj_qk")
        pj.qk_copied = sem("pj_qk_copied")
        pj.split = sem("pj_split")
        pj.part2 = sem("pj_part2")
        pj.part3 = sem("pj_part3")
        pj.parts_out0 = sem("pj_parts_out0")
        pj.parts_out1 = sem("pj_parts_out1")
        pj.parts_out2 = sem("pj_parts_out2")
        pj.parts_out3 = sem("pj_parts_out3")
        pj.parts_out = [pj.parts_out0, pj.parts_out1, pj.parts_out2, pj.parts_out3]
        pj.v = sem("pj_v")
        pj.v_copied = sem("pj_v_copied")
        pj.v_out0 = sem("pj_v_out0")
        pj.v_out1 = sem("pj_v_out1")
        a = Named()
        a.k_in = sem("a_k_in")
        a.st = sem("a_st")
        a.exp = sem("a_exp")
        a.pv = sem("a_pv")
        a.m = sem("a_m")
        a.mx = sem("a_mx")
        a.fin = sem("a_fin")
        a.mp = sem("a_mp")
        a.mt = sem("a_mt")
        a.qrow = sem("a_qrow")
        a.o_copied = sem("a_o_copied")
        a.sums_out = sem("a_sums_out")
        a.sums_in = sem("a_sums_in")
        a.recips_out = sem("a_recips_out")
        a.recips_in = sem("a_recips_in")
        a.recip = sem("a_recip")
        a.normed = sem("a_normed")
        a.at_out0 = sem("a_at_out0")
        a.at_out1 = sem("a_at_out1")
        a.v_in0 = sem("a_v_in0")
        a.v_in1 = sem("a_v_in1")
        a.rows_in = sem("a_rows_in")
        a.pm_set = sem("a_pm_set")
        a.q_in0 = sem("a_q_in0")
        a.q_in1 = sem("a_q_in1")
        a.q_in2 = sem("a_q_in2")
        a.q_in3 = sem("a_q_in3")
        a.q_in = [a.q_in0, a.q_in1, a.q_in2, a.q_in3]
        a.v_in = [a.v_in0, a.v_in1]
        a.at_out = [a.at_out0, a.at_out1]

        S = Named()
        S.nc = nc
        S.m = m
        S.ins = ins
        S.out = out
        S.exb = exb
        S.tb = tb
        S.gb = gb
        S.rb = rb
        S.mb = mb
        S.ob = ob
        S.xb = xb
        S.es = pair
        S.x1_d = x1_d
        S.qk_d = qk_d
        S.v_d = v_d
        S.at_d = at_d
        S.sums_d = sums_d
        S.recips_d = recips_d
        S.f1 = f1
        S.f2 = f2
        S.pj = pj
        S.a = a
        S.wait_value = {}
        S.consts_in = consts_in
        S.ident_in = ident_in
        S.ones_set = ones_set
        S.phase_end = phase_end

        block = ctx.enter_context(nc.Block())

        def phases(eng, name, parts):
            S.wait_value[eng] = eng.alloc_register(f"{name}_wait_value")
            for n, part in enumerate(parts):
                if n > 1:
                    eng.wait_ge(phase_end, 5 * (n - 1))
                part(eng, S)
                if 0 < n < len(parts) - 1:
                    eng.drain().then_inc(phase_end, 1)

        @block.sync
        def _(sp):
            phases(sp, "sp", [ffn1_dma, project_dma, attend_dma, ffn2_dma])

        @block.tensor
        def _(pe):
            phases(pe, "pe", [ffn1_pe, project_pe, attend_pe, ffn2_pe])

        @block.scalar
        def _(act):
            phases(act, "act", [ffn1_act, project_act, attend_act, ffn2_act])

        @block.vector
        def _(dve):
            phases(dve, "dve", [ffn1_dve, project_dve, attend_dve, ffn2_dve])

        @block.gpsimd
        def _(pool):
            phases(pool, "pool", [ffn1_pool, project_pool, attend_pool, ffn2_pool])


def wait_alone(eng, S, sem, value):
    if isinstance(value, int):
        eng.wait_ge(sem, value)
        return
    eng.reg_mov(S.wait_value[eng], value)
    eng.wait_ge(S.consts_in, 16)
    eng.wait_ge(sem, S.wait_value[eng])



def norm_stats_dve(dve, S, s, G, u, ready):
    m = S.m
    ready()
    for t in range(GT):
        dve.bn_stats(m.bst[:, 6 * t:6 * t + 6], m.xs[:, ds((G * GT + t) * D, D)]).then_inc(s.stats, 1)
    wait_alone(dve, S, s.stats, 2 * GT * G + GT)
    for t in range(GT):
        dve.bn_aggr(m.mv[u][:, 2 * t:2 * t + 2], m.bst[:, 6 * t:6 * t + 6]).then_inc(s.stats, 1)


def norm_std_act(act, S, s, G, u):
    m = S.m
    act.wait_ge(s.stats, 2 * GT * G + 2 * GT)
    act.activation(m.std[:, :], m.mv[u][:, 1:2 * GT:2], ACT.Sqrt, bias=m.eps[:, :]).then_inc(s.std, 1)


def norm_apply_dve(dve, S, s, G, u):
    m = S.m
    dve.wait_ge(s.std, G + 1)
    dve.reciprocal(m.rstd[:, :], m.std[:, :]).then_inc(s.rstd, 1)
    dve.wait_ge(s.rstd, G + 1)
    if not (isinstance(G, int) and G < 2):
        dve.wait_ge(s.turned, KD * (G - 1))
    for t in range(GT):
        dve.tensor_scalar(m.xh[u][:, t * D:(t + 1) * D], m.xs[:, ds((G * GT + t) * D, D)],
                          m.mv[u][:, 2 * t:2 * t + 1], m.rstd[:, t:t + 1], ALU.subtract, ALU.mult).then_inc(s.xhat, 1)


def turn_pe(pe, S, s, G, u, free):
    m = S.m
    pe.wait_ge(s.xhat, GT * (G + 1))
    free()
    for k in range(KD):
        for t in range(GT):
            last = pe.transpose(S.tb[k][:, t * P:(t + 1) * P], m.xh[u][:, t * D + k * P:t * D + (k + 1) * P],
                                m.ident[:, :])
        last.then_inc(s.turned, 1)


def turn_hi_act(act, S, s, G, u, free):
    m = S.m
    free()
    for k in range(KD):
        act.wait_ge(s.turned, KD * G + k + 1)
        act.activation(m.xt_hi[u][:, k * GW:(k + 1) * GW], S.tb[k][:, :], ACT.Copy).then_inc(s.hi, 1)


def turn_lo_dve(dve, S, s, G, u):
    m = S.m
    for k in range(KD):
        dve.wait_ge(s.hi, KD * G + k + 1)
        dve.tensor_tensor(m.xt_lo[u][:, k * GW:(k + 1) * GW], S.tb[k][:, :],
                          m.xt_hi[u][:, k * GW:(k + 1) * GW].bitcast(fp32), ALU.subtract).then_inc(s.lo, 1)


def split_product(pe, out, hi, lo, w_hi, w_lo, tiles):
    n = 3 * len(tiles)
    i = 0
    for k in tiles:
        for lhs, rhs in ((hi(k), w_hi(k)), (lo(k), w_hi(k)), (hi(k), w_lo(k))):
            last = pe.matmul(out, lhs, rhs, start=(i == 0), stop=(i == n - 1))
            i += 1
    return last



def groups(eng, body):
    body(0, 0, True, True)
    body(1, 1, True, True)
    with eng.Fori(1, NG // 2 - 1) as gp:
        body(2 * gp, 0, True, True)
        body(2 * gp + 1, 1, True, True)
    body(NG - 2, 0, True, False)
    body(NG - 1, 1, False, False)


def load_gate_weights(sp, S, s):
    m, ins = S.m, S.ins
    sp.dma_start(m.g_raw[:, :].rearrange("p (k e) -> p k e", k=KD),
                 ins["gate_wT"].rearrange("(k p) e -> p k e", p=P)).then_inc(s.w_in, 16)
    sp.dma_start(m.gb[0:E, :], ins["gate_b"].rearrange("(e a) -> e a", a=1)).then_inc(s.w_in, 16)
    sp.dma_start(m.eb[0:E, :], ins["expert_b"]).then_inc(s.w_in, 16)


def bank_weights(buf, n):
    return buf[:, :].rearrange("p (k c) -> p k c", k=KD)[:, :, n * EPB * D:(n + 1) * EPB * D]


def load_expert_matrices(sp, S, s):
    m, ins = S.m, S.ins
    for n in range(NB):
        for k in range(KD):
            sp.dma_start(bank_weights(m.w_raw, n)[:, k].rearrange("p (e o) -> p e o", e=EPB),
                         ins["expert_w"][n * EPB:(n + 1) * EPB, k * P:(k + 1) * P, :].rearrange("e p o -> p e o")
                         ).then_inc(s.m_in[n], 16)


W_LOADS = 16 * 3
M_LOADS = 16 * KD


def split_gates(act, dve, S, s):
    m = S.m
    if act:
        act.wait_ge(s.w_in, W_LOADS)
        act.activation(m.g_hi[:, :], m.g_raw[:, :], ACT.Copy).then_inc(s.w_hi, 1)
    if dve:
        dve.wait_ge(s.w_hi, 1)
        dve.tensor_tensor(m.g_lo[:, :], m.g_raw[:, :], m.g_hi[:, :].bitcast(fp32), ALU.subtract).then_inc(s.w_lo, 1)


def split_matrices_act(act, S, s):
    m = S.m
    for n in range(NB):
        act.wait_ge(s.m_in[n], M_LOADS)
        act.activation(bank_weights(m.w_hi, n), bank_weights(m.w_raw, n), ACT.Copy).then_inc(s.m_hi, 1)


def split_matrices_dve(dve, S, s):
    m = S.m
    for n in range(NB):
        dve.wait_ge(s.m_hi, n + 1)
        dve.tensor_tensor(bank_weights(m.w_lo, n), bank_weights(m.w_raw, n), bank_weights(m.w_hi, n).bitcast(fp32),
                          ALU.subtract).then_inc(s.m_lo, 1)


def logits_pe(pe, S, s, G, u):
    m = S.m
    pe.wait_ge(s.lo, KD * (G + 1))
    if not (isinstance(G, int) and G == 0):
        pe.wait_ge(s.gt_copied, G)
    split_product(pe, S.gb[0:E, :],
                  lambda k: m.g_hi[:, k * E:(k + 1) * E], lambda k: m.g_lo[:, k * E:(k + 1) * E],
                  lambda k: m.xt_hi[u][:, k * GW:(k + 1) * GW], lambda k: m.xt_lo[u][:, k * GW:(k + 1) * GW],
                  range(KD)).then_inc(s.lgt, 1)


def logits_copy_act(act, S, s, G):
    act.wait_ge(s.lgt, G + 1)
    act.activation(S.m.lgt[0:E, :], S.gb[0:E, :], ACT.Identity, bias=S.m.gb[0:E, :]).then_inc(s.lgt_copied, 1)


def logits_turn_pe(pe, S, s, G):
    wait_alone(pe, S, s.lgt_copied, G + 1)
    for t in range(GT):
        last = pe.transpose(S.gb[:, t * E:(t + 1) * E], S.m.lgt[0:E, t * P:(t + 1) * P], S.m.ident[0:E, 0:E])
    last.then_inc(s.lg, 1)


def gates_dve(dve, S, s, G, u):
    m = S.m
    own = 10 * G
    dve.wait_ge(s.lg, G + 1)
    dve.tensor_copy(m.lg[:, :], S.gb[:, 0:GT * E]).then_inc(s.soft, 1)
    lg = m.lg[:, :].rearrange("p (t e) -> p t e", t=GT)
    dve.wait_ge(s.soft, own + 1)
    dve.tensor_reduce(m.top[:, :], lg, axis=AX.X, op=ALU.max).then_inc(s.soft, 1)
    other = lg.unsqueeze(2).broadcast_to([P, GT, E, E])
    this = lg.unsqueeze(3).broadcast_to([P, GT, E, E])
    gtr = m.gtr[:, :].rearrange("p (t e f) -> p t e f", t=GT, e=E)
    eqr = m.eqr[:, :].rearrange("p (t e f) -> p t e f", t=GT, e=E)
    tri = m.tri[:, :].rearrange("p (e f) -> p e f", e=E).unsqueeze(1).broadcast_to([P, GT, E, E])
    dve.wait_ge(s.soft, own + 2)
    dve.tensor_tensor(m.dl[:, :].rearrange("p (t e) -> p t e", t=GT), lg,
                      m.top[:, :].unsqueeze(2).broadcast_to([P, GT, E]), ALU.subtract).then_inc(s.shifted, 1)
    dve.tensor_tensor(eqr, other, this, ALU.is_equal).then_inc(s.soft, 1)
    dve.tensor_tensor(gtr, other, this, ALU.is_gt).then_inc(s.soft, 1)
    dve.wait_ge(s.soft, own + 3)
    dve.tensor_tensor(eqr, eqr, tri, ALU.mult).then_inc(s.soft, 1)
    dve.wait_ge(s.soft, own + 5)
    dve.tensor_tensor(m.gtr[:, :], m.gtr[:, :], m.eqr[:, :], ALU.add).then_inc(s.soft, 1)
    dve.wait_ge(s.soft, own + 6)
    dve.tensor_reduce(m.rank[:, :], gtr, axis=AX.X, op=ALU.add).then_inc(s.soft, 1)
    dve.wait_ge(s.soft, own + 7)
    dve.wait_ge(s.ex, G + 1)
    dve.scalar_tensor_tensor(m.rank[:, :], m.rank[:, :], 1.5, m.ex[:, :], ALU.is_lt, ALU.mult).then_inc(s.soft, 1)
    dve.wait_ge(s.soft, own + 8)
    rank = m.rank[:, :].rearrange("p (t e) -> p t e", t=GT)
    dve.tensor_reduce(m.gsum[:, :], rank, axis=AX.X, op=ALU.add).then_inc(s.soft, 1)
    dve.wait_ge(s.soft, own + 9)
    dve.reciprocal(m.grec[:, :], m.gsum[:, :]).then_inc(s.soft, 1)
    dve.wait_ge(s.soft, own + 10)
    dve.scalar_tensor_tensor(m.gates[u][:, :].rearrange("p (t e) -> p t e", t=GT), rank, 0.5,
                             m.grec[:, :].unsqueeze(2).broadcast_to([P, GT, E]), ALU.mult, ALU.mult).then_inc(s.gates, 1)


def gates_exp_act(act, S, s, G):
    act.wait_ge(s.shifted, G + 1)
    act.activation(S.m.ex[:, :], S.m.dl[:, :], ACT.Exp).then_inc(s.ex, 1)


def gates_turn_pe(pe, S, s, G, u):
    pe.wait_ge(s.gates, G + 1)
    for t in range(GT):
        last = pe.transpose(S.gb[0:E, t * P:(t + 1) * P], S.m.gates[u][:, t * E:(t + 1) * E], S.m.ident[:, :])
    last.then_inc(s.gt, 1)


def gates_copy_act(act, S, s, G, u):
    act.wait_ge(s.gt, G + 1)
    if not (isinstance(G, int) and G == 0):
        act.wait_ge(s.bias, GT * (G - 1))
    act.activation(S.m.gts[u][0:E, :], S.gb[0:E, :], ACT.Copy).then_inc(s.gt_copied, 1)


def experts_pe(pe, S, s, G, u, t):
    m = S.m
    T = G * GT + t
    if t == 0:
        pe.wait_ge(s.gt_copied, G + 1)
    if not (isinstance(T, int) and T == 0):
        pe.wait_ge(s.acc_set, T)
    pe.matmul(S.rb[:, 0:D], m.gts[u][0:E, t * P:(t + 1) * P], m.eb[0:E, :], start=True, stop=True).then_inc(s.bias, 1)
    for n in range(NB):
        if isinstance(T, int) and T == 0:
            pe.wait_ge(s.m_lo, n + 1)
        pe.wait_ge(s.used, E * T + EPB * (n + 1))
        split_product(pe, S.exb[n],
                      lambda k: m.xt_hi[u][:, k * GW + t * P:k * GW + (t + 1) * P],
                      lambda k: m.xt_lo[u][:, k * GW + t * P:k * GW + (t + 1) * P],
                      lambda k: m.w_hi[:, k * E * D + n * 512:k * E * D + (n + 1) * 512],
                      lambda k: m.w_lo[:, k * E * D + n * 512:k * E * D + (n + 1) * 512],
                      range(KD)).then_inc(s.experts, 1)


def bias_act(act, S, s, G, t):
    T = G * GT + t
    act.wait_ge(s.bias, T + 1)
    act.wait_ge(s.added, T + 1)
    act.activation(S.m.acc[t % 2][:, :], S.rb[:, 0:D], ACT.Copy).then_inc(s.acc_set, 1)


def experts_dve(dve, S, s, G, u, t):
    m = S.m
    T = G * GT + t
    x = m.xs[:, ds(T * D, D)]
    acc = m.acc[t % 2][:, :]
    dve.wait_ge(s.acc_set, T + 1)
    for n in range(NB):
        dve.wait_ge(s.experts, NB * T + n + 1)
        for i, into in enumerate((x, acc)):
            e = EPB * n + i
            if n:
                dve.wait_ge(s.used, E * T + E + e - 1)
            dve.scalar_tensor_tensor(into, S.exb[n][:, i * D:(i + 1) * D], m.gates[u][:, t * E + e:t * E + e + 1],
                                     into, ALU.mult, ALU.add).then_inc(s.used, 1)


def add_pool(pool, S, s, G, t):
    T = G * GT + t
    x = S.m.xs[:, ds(T * D, D)]
    pool.wait_ge(s.used, E * T + 2 * E)
    pool.tensor_tensor(x, x, S.m.acc[t % 2][:, :], ALU.add).then_inc(s.added, 1)


def ffn_pe(pe, S, s, free_tb, also, turn_after=None, second=None):
    turn_pe(pe, S, s, 0, 0, lambda: free_tb(0))
    pe.wait_ge(s.w_lo, 1)
    logits_pe(pe, S, s, 0, 0)
    logits_turn_pe(pe, S, s, 0)
    if second:
        second()
    gates_turn_pe(pe, S, s, 0, 0)

    def body(G, u, nxt, nxt2):
        experts_pe(pe, S, s, G, u, 0)
        if nxt:
            turn_pe(pe, S, s, G + 1, 1 - u, lambda: free_tb(G + 1))
        elif turn_after:
            turn_after()
        experts_pe(pe, S, s, G, u, 1)
        if nxt:
            logits_pe(pe, S, s, G + 1, 1 - u)
        experts_pe(pe, S, s, G, u, 2)
        if nxt:
            logits_turn_pe(pe, S, s, G + 1)
        experts_pe(pe, S, s, G, u, 3)
        if nxt:
            gates_turn_pe(pe, S, s, G + 1, 1 - u)
        if nxt2:
            also(G + 2, u)

    groups(pe, body)


def ffn_act(act, S, s, also, second, turn_after=None, norm_after=None):
    def free_xt(G):
        if not (isinstance(G, int) and G == 0):
            act.wait_ge(s.experts, GT * NB * (G - 1))
    turn_hi_act(act, S, s, 0, 0, lambda: free_xt(0))
    logits_copy_act(act, S, s, 0)
    gates_exp_act(act, S, s, 0)
    gates_copy_act(act, S, s, 0, 0)
    second()

    def body(G, u, nxt, nxt2):
        bias_act(act, S, s, G, 0)
        if nxt:
            turn_hi_act(act, S, s, G + 1, 1 - u, lambda: free_xt(G + 1))
        elif turn_after:
            turn_after()
        if nxt2:
            also(G + 2, u)
        bias_act(act, S, s, G, 1)
        if nxt:
            logits_copy_act(act, S, s, G + 1)
        bias_act(act, S, s, G, 2)
        if nxt:
            gates_exp_act(act, S, s, G + 1)
        bias_act(act, S, s, G, 3)
        if nxt:
            gates_copy_act(act, S, s, G + 1, 1 - u)
        if nxt2:
            norm_std_act(act, S, s, G + 2, u)
        elif norm_after:
            norm_after(u)

    groups(act, body)


def ffn_dve(dve, S, s, ready, second, turn_after=None, norm_after=None):
    turn_lo_dve(dve, S, s, 0, 0)
    gates_dve(dve, S, s, 0, 0)
    second()

    def body(G, u, nxt, nxt2):
        experts_dve(dve, S, s, G, u, 0)
        if nxt:
            turn_lo_dve(dve, S, s, G + 1, 1 - u)
        elif turn_after:
            turn_after()
        experts_dve(dve, S, s, G, u, 1)
        experts_dve(dve, S, s, G, u, 2)
        if nxt:
            gates_dve(dve, S, s, G + 1, 1 - u)
        experts_dve(dve, S, s, G, u, 3)
        if nxt2:
            norm_stats_dve(dve, S, s, G + 2, u, lambda: ready(G + 2, u))
            norm_apply_dve(dve, S, s, G + 2, u)
        elif norm_after:
            norm_after(u)

    groups(dve, body)


def ffn_pool(pool, S, s, also):
    def body(G, u, nxt, nxt2):
        for t in range(GT):
            add_pool(pool, S, s, G, t)
            if nxt2:
                also(G + 2, u, t)
    groups(pool, body)


def store_groups(sp, S, s, dst, also):
    stored = (s.stored0, s.stored1)
    rows = dst.rearrange("(n p) d -> p n d", p=P)

    def body(G, u, nxt, nxt2):
        if nxt2:
            also(G + 2, u)
        sp.wait_ge(s.added, GT * (G + 1) + 2)
        if not (isinstance(G, int) and G < 2):
            sp.wait_ge(stored[u], 16 * (G // 2 if isinstance(G, int) else (G - u) // 2))
        sp.dma_start(rows[:, ds(G * GT, GT), :],
                     S.m.xs[:, ds(G * GT * D, GT * D)].rearrange("p (n d) -> p n d", d=D)).then_inc(stored[u], 16)
    groups(sp, body)
    for u in range(2):
        sp.wait_ge(stored[u], 16 * NG // 2)



def load_projection_weights(sp, S):
    m, ins, s = S.m, S.ins, S.pj
    for i, name in enumerate(("WqT", "WkT", "WvT")):
        sp.dma_start(m.qkv_raw[:, :].rearrange("p (w k e) -> p w k e", w=3, k=KD)[:, i],
                     ins[name].rearrange("(k p) e -> p k e", p=P)).then_inc(s.w_in, 16)
    for i, name in enumerate(("bq", "bk")):
        sp.dma_start(m.qk_bias[:, 2 * i:2 * i + 2], ins[name].rearrange("(k p) -> p k", p=P),
                     allow_slow_non_contiguous=True).then_inc(s.w_in, 16)
    sp.dma_start(m.v_bias[:, :], ins["bv"].rearrange("(a n) -> a n", a=1).broadcast_to([P, D])).then_inc(s.w_in, 16)


def ffn1_dma(sp, S):
    m, ins, s = S.m, S.ins, S.f1
    x_rows = ins["x"].rearrange("(n p) d -> p n d", p=P)
    x_in = (s.x_in0, s.x_in1)

    def load_x(G, u):
        if not (isinstance(G, int) and G < 2):
            sp.wait_ge(x_in[u], 16 * (G // 2 if isinstance(G, int) else (G - u) // 2))
        sp.dma_start(m.xs[:, ds(G * GT * D, GT * D)].rearrange("p (n d) -> p n d", d=D),
                     x_rows[:, ds(G * GT, GT), :]).then_inc(x_in[u], 16)

    sp.dma_start(m.ident[:, :], ins["c_ident"]).then_inc(S.ident_in, 16)
    load_x(0, 0)
    load_x(1, 1)
    load_gate_weights(sp, S, s)
    for name, dst in (("c_ident16", m.ident16), ("c_tri", m.tri), ("c_mask_q", m.mask_q),
                      ("c_mask_k", m.mask_k), ("c_off", m.off), ("c_mparts", m.mparts)):
        sp.dma_start(dst[:, :], ins[name]).then_inc(S.consts_in, 16)
    load_expert_matrices(sp, S, s)
    load_projection_weights(sp, S)
    store_groups(sp, S, s, S.x1_d, load_x)


CONST_LOADS = 16 * 6


def ffn1_pe(pe, S):
    s = S.f1
    pe.wait_ge(S.ident_in, 16)

    def free_tb(G):
        if not (isinstance(G, int) and G == 0):
            pe.wait_ge(s.lo, KD * G)
    ffn_pe(pe, S, s, free_tb, lambda G, u: None,
           lambda: turn_pe(pe, S, S.pj, 0, 0, lambda: pe.wait_ge(s.lo, KD * NG)))


def ffn1_act(act, S):
    s = S.f1
    act.wait_ge(S.ones_set, 1)
    norm_std_act(act, S, s, 0, 0)
    norm_std_act(act, S, s, 1, 1)
    split_gates(act, None, S, s)
    pj = S.pj

    def also(G, u):
        if isinstance(G, int) and G == 3:
            act.wait_ge(pj.w_in, PJ_LOADS)
            act.activation(S.m.qkv_hi[:, :], S.m.qkv_raw[:, :], ACT.Copy).then_inc(pj.w_hi, 1)
    ffn_act(act, S, s, also, lambda: split_matrices_act(act, S, s),
            lambda: turn_hi_act(act, S, pj, 0, 0, lambda: act.wait_ge(s.experts, GT * NB * (NG - 1))),
            lambda u: norm_std_act(act, S, pj, u, u))


def ffn1_dve(dve, S):
    s = S.f1
    x_in = (s.x_in0, s.x_in1)
    dve.memset(S.m.eps[:, :], EPS).then_inc(S.ones_set, 1)
    dve.memset(S.m.zero16[:, :], 0.0).then_inc(S.ones_set, 1)
    dve.sem_inc(s.used, E)

    def ready(G, u):
        wait_alone(dve, S, x_in[u], 16 * (G // 2 + 1 if isinstance(G, int) else (G - u) // 2 + 1))
    for G in range(2):
        norm_stats_dve(dve, S, s, G, G, lambda: ready(G, G))
        norm_apply_dve(dve, S, s, G, G)
    split_gates(None, dve, S, s)
    dve.wait_ge(S.consts_in, CONST_LOADS)
    pj, m = S.pj, S.m

    def ready_and_weights(G, u):
        ready(G, u)
        if isinstance(G, int) and G == 3:
            dve.wait_ge(pj.w_hi, 1)
            dve.tensor_scalar(m.qk_bias[:, 0:2], m.qk_bias[:, 0:2], 0.25, None, ALU.mult)
            dve.tensor_tensor(m.qkv_lo[:, :], m.qkv_raw[:, :], m.qkv_hi[:, :].bitcast(fp32),
                              ALU.subtract).then_inc(pj.w_lo, 1)

    def norm_after(u):
        norm_stats_dve(dve, S, pj, u, u, lambda: dve.wait_ge(s.added, GT * (u + 1) + 2))
        dve.wait_ge(s.turned, KD * (NG - 1 + u))
        norm_apply_dve(dve, S, pj, u, u)
    ffn_dve(dve, S, s, ready_and_weights, lambda: split_matrices_dve(dve, S, s), lambda: turn_lo_dve(dve, S, pj, 0, 0), norm_after)


def ffn1_pool(pool, S):
    pool.sem_inc(S.f1.added, 2)
    for u in range(2):
        pool.memset(S.m.vpad[u][:, :], 1.0).then_inc(S.ones_set, 1)
    ffn_pool(pool, S, S.f1, lambda G, u, t: None)



def project_dma(sp, S):
    m, s = S.m, S.pj
    v_out = (s.v_out0, s.v_out1)
    sp.dma_start(m.Q[KR:KR + AR + MR, :], S.ins["c_qrows"]).then_inc(S.a.rows_in, 16)

    def body(G, u, nxt, nxt2):
        for i in range(4):
            sp.wait_ge(s.part3, 4 * G + i + 1)
            sp.dma_start(S.qk_d[i // 2, :, (i % 2) * P:(i % 2 + 1) * P, ds(G * GW, GW)].rearrange("c p t -> p c t"),
                         m.parts[i][:, :].rearrange("p (c t) -> p c t", c=3)).then_inc(s.parts_out[i], 16)
        sp.wait_ge(s.v_copied, 2 * (G + 1) + 2)
        for t in range(GT):
            sp.dma_start(S.v_d[:, ds(G * GT + t, 1), :, :].rearrange("g n p f -> p (g n) f"),
                         m.vpad[u][:, t * 512:(t + 1) * 512].rearrange("p (g f) -> p g f", g=NHG)).then_inc(v_out[u], 16)
        if isinstance(G, int) and G == 1:
            for i in range(4):
                sp.wait_ge(s.parts_out[i], 16)
            for hg in range(NHG):
                load_queries(sp, S, 0, hg)
    groups(sp, body)
    for i in range(4):
        sp.wait_ge(s.parts_out[i], 16 * NG)
    for u in range(2):
        sp.wait_ge(v_out[u], 16 * GT * NG // 2)


PJ_LOADS = 16 * 6


def project_pe(pe, S):
    m, s = S.m, S.pj

    def free_tb(G):
        if not (isinstance(G, int) and G == 0):
            pe.wait_ge(s.lo, KD * G)
    pe.wait_ge(s.w_lo, 1)
    pe.wait_ge(S.f1.acc_set, GT * NG)

    def body(G, u, nxt, nxt2):
        pe.wait_ge(s.lo, KD * (G + 1))
        for i in range(4):
            if i == 2 and nxt:
                turn_pe(pe, S, s, G + 1, 1 - u, lambda: free_tb(G + 1))
            pe.wait_ge(s.qk_copied, 4 * G + i + 1)
            w = (i // 2) * KD * D + (i % 2) * P
            split_product(pe, S.exb[i],
                          lambda k: m.qkv_hi[:, w + k * D:w + k * D + P], lambda k: m.qkv_lo[:, w + k * D:w + k * D + P],
                          lambda k: m.xt_hi[u][:, k * GW:(k + 1) * GW], lambda k: m.xt_lo[u][:, k * GW:(k + 1) * GW],
                          range(KD)).then_inc(s.qk, 1)
        w = 2 * KD * D
        for t in range(GT):
            bank = (S.gb, S.rb)[t // 2]
            if t % 2 == 0:
                pe.wait_ge(s.v_copied, 2 * G + t // 2 + 1)
            last = split_product(pe, bank[:, (t % 2) * D:(t % 2 + 1) * D],
                          lambda k: m.xt_hi[u][:, k * GW + t * P:k * GW + (t + 1) * P],
                          lambda k: m.xt_lo[u][:, k * GW + t * P:k * GW + (t + 1) * P],
                          lambda k: m.qkv_hi[:, w + k * D:w + (k + 1) * D], lambda k: m.qkv_lo[:, w + k * D:w + (k + 1) * D],
                          range(KD))
            if t % 2:
                last.then_inc(s.v, 1)
    groups(pe, body)
    first_maxima_pe(pe, S)


def project_act(act, S):
    m, s = S.m, S.pj

    def free_xt(G):
        if not (isinstance(G, int) and G == 0):
            act.wait_ge(s.v, 2 * (G - 1))

    def part2(G, i):
        act.wait_ge(s.split, 4 * G + i + 1)
        act.activation(m.parts[i][:, GW:2 * GW], m.tr[i][:, :], ACT.Copy).then_inc(s.part2, 1)

    def body(G, u, nxt, nxt2):
        for i in range(4):
            if i == 2 and nxt2:
                norm_std_act(act, S, s, G + 2, u)
            if i == 2 and nxt:
                turn_hi_act(act, S, s, G + 1, 1 - u, lambda: free_xt(G + 1))
            act.wait_ge(s.qk, 4 * G + i + 1)
            if not (isinstance(G, int) and G == 0):
                act.wait_ge(s.parts_out[i], 16 * G)
            scale = 0.25 if i < 2 else 1.0
            act.activation(m.tq[i][:, :], S.exb[i][:, :], ACT.Identity, bias=m.qk_bias[:, i:i + 1], scale=scale)
            act.activation(m.parts[i][:, 0:GW], S.exb[i][:, :], ACT.Identity, bias=m.qk_bias[:, i:i + 1],
                           scale=scale).then_inc(s.qk_copied, 1)
            if i >= 2:
                part2(G, i - 2)
        part2(G, 2)
        part2(G, 3)
    groups(act, body)
    for j in range(HG):
        shift_row_act(act, S, 0, 0, j)


def project_pool(pool, S):
    m, s = S.m, S.pj

    def body(G, u, nxt, nxt2):
        for i in range(4):
            pool.wait_ge(s.qk_copied, 4 * G + i + 5)
            pool.tensor_tensor(m.tr[i][:, :], m.tq[i][:, :], m.parts[i][:, 0:GW],
                               ALU.subtract).then_inc(s.split, 1)
        if isinstance(G, int) and G == 1:
            pool.wait_ge(S.f1.m_lo, NB)
            for i in range(2, 4):
                pool.wait_ge(s.parts_out[i], 16)
            load_keys(pool, S, 0)
    groups(pool, body)


def project_dve(dve, S):
    m, s = S.m, S.pj
    v_out = (s.v_out0, s.v_out1)
    dve.wait_ge(S.f1.used, E * GT * NG + E)
    dve.sem_inc(s.qk_copied, 4)
    dve.sem_inc(s.v_copied, 2)
    dve.wait_ge(S.f1.added, GT * NG + 2)
    dve.wait_ge(S.ones_set, 4)

    def body(G, u, nxt, nxt2):
        def part3(i):
            dve.wait_ge(s.part2, 4 * G + i + 1)
            dve.tensor_tensor(m.parts[i][:, 2 * GW:3 * GW], m.tr[i][:, :], m.parts[i][:, GW:2 * GW],
                              ALU.subtract).then_inc(s.part3, 1)

        if nxt2:
            norm_stats_dve(dve, S, s, G + 2, u, lambda: None)
        if nxt:
            turn_lo_dve(dve, S, s, G + 1, 1 - u)
        part3(0)
        part3(1)
        if nxt2:
            norm_apply_dve(dve, S, s, G + 2, u)
        if not (isinstance(G, int) and G < 2):
            dve.wait_ge(v_out[u], 16 * GT * (G // 2 if isinstance(G, int) else (G - u) // 2))
        for h in range(2):
            dve.wait_ge(s.v, 2 * G + h + 1)
            bank = (S.gb, S.rb)[h]
            for t in range(2):
                ins = dve.tensor_tensor(
                    m.vpad[u][:, (2 * h + t) * 512:(2 * h + t + 1) * 512].rearrange("p (h d) -> p h d", h=H)[:, :, 0:HD],
                    bank[:, t * D:(t + 1) * D].rearrange("p (h d) -> p h d", h=H),
                    m.v_bias[:, :].rearrange("p (h d) -> p h d", h=H), ALU.add)
            ins.then_inc(s.v_copied, 1)
        part3(2)
        part3(3)
        if not nxt:
            first_maxima_dve(dve, S)
    groups(dve, body)



def index(qb, hg, kc):
    return 2 * qb * (qb + 1) + hg * (qb + 1) + kc


def q_blocks(eng, body):
    body(0)
    body(1)
    with eng.Fori(2, NQB - 1) as qb:
        body(qb)
    body(NQB - 1)


def chunks(eng, qb, body):
    if isinstance(qb, int) and qb == 0:
        body(0, True, True)
        return
    body(0, True, False)
    if not (isinstance(qb, int) and qb == 1):
        with eng.Fori(1, qb) as kc:
            body(kc, False, False)
    body(qb, False, True)


def maxima_of(qb, hg):
    if hg < 2:
        return qb, hg + 2
    if isinstance(qb, int) and qb == NQB - 1:
        return None
    return qb + 1, hg - 2


def step_after(qb, hg):
    if hg < NHG - 1:
        return qb, hg + 1
    if isinstance(qb, int) and qb == NQB - 1:
        return None
    return qb + 1, 0


def scores_pe(pe, S, qb, hg, kc, diag, idx):
    m, a = S.m, S.a
    half, j = idx // HG, idx % HG
    out = S.es[idx % 2]
    pe.wait_ge(a.exp, 8 * index(qb, hg, kc) + idx + 1)
    for b in range(2):
        c = 2 * half + b
        q0 = c * P if diag else 0
        last = pe.matmul(out[:, b * 512 + q0:(b + 1) * 512],
                         m.K[0:KR + AR + MR, ds(kc * H * QB + (hg * HG + j) * QB + c * P, P)],
                         m.Q[0:KR + AR + MR, (hg * HG + j) * QB + q0:(hg * HG + j + 1) * QB], start=True, stop=not diag)
        if diag:
            last = pe.matmul(out[:, b * 512 + q0:b * 512 + q0 + P], m.ident16[:, :], m.mask_k[:, :], start=False, stop=True)
    last.then_inc(a.st, 1)


FIRST_ORDER = ("M S0 M S1 M P0 M S2 M M S3 M P1 S4 M M S5 M R M P2 "
               "M S6 M M S7 M P3 M").split()
ORDER = ("S0 S1 M M M P0 M S2 M S3 M M P1 M M S4 S5 M M P2 "
         "M M S6 M S7 M P3 M").split()
DOUBLE_ORDER = ("M M M S0 M M M S1 M M P0 M M S2 M M M M S3 M M P1 "
                "M M S4 M M S5 M M M M P2 M M M S6 M M M M M P3 S7").split()


def maxima_tiles(mx, hg, kc, diag):
    if diag and hg >= 2:
        return [t for i in range(16) for t in ((i, mx[0], True), (i, kc, False))]
    return [(i, kc, diag) for i in range(16)]


def maxima_bank(r, tiles, wide):
    return r % 2 if not wide else 1 if (r, tiles) == (15, 16) else r % 3


def maxima_pe(pe, S, mx, kc0, r, tiles, wide):
    m, a = S.m, S.a
    qb, hg = mx
    i, kc, diag = tiles[r]
    j, qs = i // 4, i % 4
    h = hg * HG + j
    w = (qs + 1) * P if diag else QB
    still_open = 2 if wide and r >= 2 and (r, len(tiles)) != (15, 16) else 1
    pe.wait_ge(a.mx, 16 * index(qb, hg, kc0) + r - still_open + 3)
    bank = S.mb[maxima_bank(r, len(tiles), wide)]
    last = pe.matmul(bank[:, 0:w], m.Q[0:KR + AR, h * QB + qs * P:h * QB + (qs + 1) * P],
                     m.K[0:KR + AR, ds(kc * H * QB + h * QB, w)], start=True, stop=not diag)
    if diag:
        last = pe.matmul(bank[:, w - P:w], m.ident16[:, :], m.mask_q[:, :], start=False, stop=True)
    last.then_inc(a.m, 1)


def maxima_begin_pe(pe, S, qb, hg):
    pe.wait_ge(S.a.q_in[hg], 16 * 6 * (qb + 1))
    if hg == 0:
        pe.wait_ge(S.a.k_in, 16 * K_LOADS * (qb + 1))


def values_pe(pe, S, half, b, diag, last_inc):
    m = S.m
    c = 2 * half + b
    q0 = c * P if diag else 0
    for j in range(HG):
        last = pe.matmul(S.ob[32 * j:32 * j + 32, q0:512], m.V[half][:, b * P + 32 * j:b * P + 32 * j + 32],
                         m.prob[half][:, (2 * j + b) * QB + q0:(2 * j + b + 1) * QB], start=False, stop=True,
                         skip_group_check=True)
    if last_inc:
        last.then_inc(S.a.pv, 1)


def shift_rows_pe(pe, S, s_next, hg):
    m, a = S.m, S.a
    pe.wait_ge(a.mp, s_next + 1)
    for j in range(HG):
        for qs in range(4):
            c = ((hg * HG + j) * 4 + qs) * (AR + MR)
            last = pe.matmul(S.xb[32 * j:32 * j + AR + MR, qs * P:(qs + 1) * P], m.mparts[:, c:c + AR + MR],
                             m.ident16[:, :], start=True, stop=True)
    last.then_inc(a.mt, 1)


def first_maxima_pe(pe, S):
    a = S.a
    pe.wait_ge(S.pj.lo, KD * NG)
    pe.wait_ge(S.pj.v_copied, 2 * NG + 2)
    pe.wait_ge(S.consts_in, CONST_LOADS)
    pe.sem_inc(a.mx, 3)
    pe.wait_ge(a.rows_in, 16)
    for hg in range(2):
        maxima_begin_pe(pe, S, 0, hg)
        for i in range(16):
            maxima_pe(pe, S, (0, hg), 0, i, maxima_tiles((0, hg), 0, 0, True), False)
    shift_rows_pe(pe, S, 0, 0)


def attend_pe(pe, S):
    m, a = S.m, S.a
    pe.sem_inc(a.exp, 2)
    pe.sem_inc(a.pv, 1)

    def step(qb, hg):
        s = NHG * qb + hg
        is_first = isinstance(s, int) and s == 0
        mx = maxima_of(qb, hg)
        nxt = step_after(qb, hg)
        if mx:
            maxima_begin_pe(pe, S, *mx)
        else:
            pe.wait_ge(a.mx, 16 * index(NQB, 0, 0) + 3)
        pe.wait_ge(a.qrow, HG * (s + 1))

        def chunk(kc, first, diag):
            n = index(qb, hg, kc)
            tiles = maxima_tiles(mx, hg, kc, diag) if mx else []
            order = FIRST_ORDER if first else DOUBLE_ORDER if len(tiles) == 32 else ORDER
            each = len(tiles) // order.count("M")
            r = 0
            for part in order:
                what, i = part[0], int(part[1:] or 0)
                if what == "S":
                    scores_pe(pe, S, qb, hg, kc, diag, i)
                elif what == "M":
                    for _ in range(each):
                        if r == 2 and not first and nxt:
                            pe.wait_ge(a.qrow, HG * (s + 2))
                        maxima_pe(pe, S, mx, kc, r, tiles, not first)
                        r += 1
                elif what == "R":
                    if nxt:
                        shift_rows_pe(pe, S, s + 1, nxt[1])
                elif i < 2:
                    if not (is_first and first):
                        if i == 0:
                            pe.wait_ge(a.exp, 8 * n + 2)
                            pe.wait_ge(a.v_in[1], 16 * n)
                        values_pe(pe, S, 1, i, first, i == 1)
                else:
                    if i == 2:
                        if first:
                            if not is_first:
                                pe.wait_ge(a.o_copied, s)
                            pe.matmul(S.ob[:, :], m.zero16[:, 0:P], m.zero16[:, :], start=True, stop=True)
                        pe.wait_ge(a.exp, 8 * n + 4 + 2)
                        pe.wait_ge(a.v_in[0], 16 * (n + 1))
                    values_pe(pe, S, 0, i - 2, diag, i == 3)

        chunks(pe, qb, chunk)

    q_blocks(pe, lambda qb: [step(qb, hg) for hg in range(NHG)])
    n = index(NQB - 1, NHG - 1, NQB)
    pe.wait_ge(a.exp, 8 * n + 2)
    pe.wait_ge(a.v_in[1], 16 * n)
    for b in range(2):
        values_pe(pe, S, 1, b, True, b == 1)


def shift_row_act(act, S, s_next, hg, j):
    m, a = S.m, S.a
    h = hg * HG + j
    if j == 0:
        act.wait_ge(a.mt, s_next + 1)
    act.activation(m.Q[KR:KR + AR + MR, h * QB:(h + 1) * QB], S.xb[32 * j:32 * j + AR + MR, :],
                   ACT.Copy).then_inc(a.qrow, 1)


def attend_act(act, S):
    m, a = S.m, S.a

    def copy_out(n, par, stored):
        act.wait_ge(a.pv, 2 * n + 1)
        if not (isinstance(stored, int) and stored == 0):
            act.wait_ge(a.at_out[par], 16 * stored)
        act.activation(m.o[par][:, :], S.ob[:, :], ACT.Copy).then_inc(a.o_copied, 1)

    def step(qb, hg):
        s = NHG * qb + hg
        nxt = step_after(qb, hg)

        def chunk(kc, first, diag):
            n = index(qb, hg, kc)
            for idx in range(8):
                half, j = idx // HG, idx % HG
                if idx % HG == 0:
                    act.wait_ge(a.pv, 2 * n + half)
                wait_alone(act, S, a.st, 8 * n + idx + 1)
                at = (hg * HG + j) * CW + (NQB - 1)
                bias = m.off[:, at:at + 1] if diag else m.off[:, ds(at - qb + kc, 1)]
                base = 2 * j * QB
                if diag:
                    for b in range(2):
                        q0 = (2 * half + b) * P
                        last = act.activation(m.prob[half][:, base + b * QB + q0:base + (b + 1) * QB],
                                              S.es[idx % 2][:, b * 512 + q0:(b + 1) * 512], ACT.Exp, bias=bias)
                else:
                    last = act.activation(m.prob[half][:, base:base + 2 * QB], S.es[idx % 2][:, :], ACT.Exp, bias=bias)
                last.then_inc(a.exp, 1)
                if first and idx == 3 and not (isinstance(s, int) and s == 0):
                    copy_out(n, (hg - 1) % 2, 2 * qb + (hg - 1) // 2)
                if first and nxt and idx >= 4:
                    shift_row_act(act, S, s + 1, nxt[1], idx - 4)
        chunks(act, qb, chunk)

    q_blocks(act, lambda qb: [step(qb, hg) for hg in range(NHG)])
    copy_out(index(NQB - 1, NHG - 1, NQB), 1, 2 * NQB - 1)


def reciprocals_dve(dve, S, s):
    m, a = S.m, S.a
    dve.wait_ge(a.sums_in, 16 * s)
    if not (isinstance(s, int) and s == 1):
        dve.wait_ge(a.recips_out, 16 * (s - 1))
    dve.reciprocal(m.recips[:, :], m.sums[:, :]).then_inc(a.recip, 1)


def split_next_weights_dve(dve, S):
    m, a, s = S.m, S.a, S.f2
    dve.wait_ge(s.wo_in, WO_LOADS)
    dve.tensor_copy(m.wo_hi[:, :], m.wo_raw[:, :]).then_inc(s.wo_hi, 1)
    dve.wait_ge(s.wo_hi, 1)
    dve.tensor_tensor(m.wo_lo[:, :], m.wo_raw[:, :], m.wo_hi[:, :].bitcast(fp32), ALU.subtract).then_inc(s.wo_lo, 1)
    n = index(NQB - 1, NHG - 1, 0)
    dve.wait_ge(a.st, 8 * (n + 2))
    for b in range(NB):
        dve.wait_ge(s.m_in[b], M_LOADS)
        dve.tensor_copy(bank_weights(m.w_hi, b), bank_weights(m.w_raw, b)).then_inc(s.m_hi, 1)
    dve.wait_ge(a.st, 8 * (n + 3))
    split_matrices_dve(dve, S, s)


def maxima_tables(S):
    return ([buf[:, :].rearrange("p (j c) -> p j c", c=NQB) for buf in S.m.pm],
            [buf[:, :].rearrange("p (j c) -> p j c", c=NQB + 1) for buf in S.m.pmo])


def finish_maxima(dve, S, qb, hg):
    m, a = S.m, S.a
    s = NHG * qb + hg
    own = 3 * s
    pm, pmo = maxima_tables(S)
    off = m.off[:, :].rearrange("p (h c) -> p h c", h=H)[:, hg * HG:(hg + 1) * HG, ds(NQB - 1 - qb, NQB)]
    parts = m.mparts[:, hg * 16 * 8:(hg + 1) * 16 * 8].rearrange("p (j c) -> p j c", c=AR + MR)

    def offsets():
        wait_alone(dve, S, a.mx, 16 * (index(qb, hg, qb) + 1) + 3)
        table = [P, HG, 4, NQB]
        dve.tensor_tensor(pmo[hg % 2].rearrange("p (j q) c -> p j q c", j=HG)[:, :, :, 0:NQB],
                          pm[hg % 2].rearrange("p (j q) c -> p j q c", j=HG),
                          off.unsqueeze(2).broadcast_to(table), ALU.add).then_inc(a.fin, 1)

    def maximum():
        dve.wait_ge(a.fin, own + 1)
        dve.tensor_reduce(m.nmax[:, :], pmo[hg % 2], axis=AX.X, op=ALU.max, negate=True).then_inc(a.fin, 1)

    def high():
        dve.wait_ge(a.fin, own + 2)
        dve.tensor_copy(parts[:, :, AR], m.nmax[:, :]).then_inc(a.fin, 1)

    def low():
        dve.wait_ge(a.fin, own + 3)
        dve.tensor_tensor(parts[:, :, AR + 1], m.nmax[:, :], parts[:, :, AR], ALU.subtract).then_inc(a.mp, 1)
    return [offsets, maximum, high, low]


def reduce_maxima(dve, S, mx, kc0, tiles, wide, between):
    m, a = S.m, S.a
    pmo = maxima_tables(S)[1]
    n = index(mx[0], mx[1], kc0)
    for r, (i, kc, diag) in enumerate(tiles):
        w = (i % 4 + 1) * P if diag else QB
        wait_alone(dve, S, a.m, 16 * n + r + 1)
        to = pmo[mx[1] % 2][:, i, NQB:NQB + 1] if diag else m.pm[mx[1] % 2][:, ds(i * NQB + kc, 1)]
        dve.tensor_reduce(to, S.mb[maxima_bank(r, len(tiles), wide)][:, 0:w], axis=AX.X, op=ALU.max).then_inc(a.mx, 1)
        if 1 <= r <= len(between):
            between[r - 1]()


def first_maxima_dve(dve, S):
    m, a = S.m, S.a
    for buf in m.pm:
        dve.memset(buf[:, :], -1.0e38).then_inc(a.pm_set, 1)
    dve.wait_ge(a.pm_set, 2)
    for hg in range(2):
        reduce_maxima(dve, S, (0, hg), 0, maxima_tiles((0, hg), 0, 0, True), False,
                      finish_maxima(dve, S, 0, 0) if hg else [])


def attend_dve(dve, S):
    m = S.m
    dve.memset(m.wo_raw[:, :], 0.0).then_inc(S.f2.wo_set, 1)

    def step(qb, hg):
        s = NHG * qb + hg
        mx = maxima_of(qb, hg)
        ended = step_after(qb, hg)

        def chunk(kc, first, diag):
            between = finish_maxima(dve, S, *ended) if first and ended else []
            if mx:
                reduce_maxima(dve, S, mx, kc, maxima_tiles(mx, hg, kc, diag), not first, between)
            elif first:
                for part in between:
                    part()
        chunks(dve, qb, chunk)
        if not (isinstance(s, int) and s == 0):
            reciprocals_dve(dve, S, s)

    q_blocks(dve, lambda qb: [step(qb, hg) for hg in range(NHG)])
    split_next_weights_dve(dve, S)


def load_queries(sp, S, qb, hg):
    for c, part in enumerate(Q_PART):
        sp.dma_start(S.m.Q[HD * c:HD * (c + 1), hg * HG * QB:(hg + 1) * HG * QB].rearrange("d (j t) -> d j t", j=HG),
                     S.qk_d[0, part, hg * HG * HD:(hg + 1) * HG * HD, ds(qb * QB, QB)].rearrange("(j d) t -> d j t", d=HD)
                     ).then_inc(S.a.q_in[hg], 16)


def attend_dma(sp, S):
    m, a = S.m, S.a
    load_output_weights(sp, S)

    def step(qb, hg):
        first = index(qb, hg, 0)
        if hg:
            if not (isinstance(qb, int) and qb == NQB - 1):
                sp.wait_ge(a.st, 8 * first)
                load_queries(sp, S, qb + 1, hg - 1)
        elif not (isinstance(qb, int) and qb == 0):
            sp.wait_ge(a.st, 8 * first)
            load_queries(sp, S, qb, NHG - 1)

        def chunk(kc, first, diag):
            n = index(qb, hg, kc)
            for half in range(2):
                sp.wait_ge(a.pv, 2 * n + half)
                sp.dma_start(m.V[half][:, :].rearrange("p (k f) -> p k f", k=2),
                             S.v_d[hg, ds(kc * 4 + 2 * half, 2), :, :].rearrange("k p f -> p k f")).then_inc(a.v_in[half], 16)
            if isinstance(qb, int) and (qb, hg) == (NQB - 1, NHG - 1) and first:
                sp.wait_ge(a.st, 8 * (n + 1))
                load_expert_matrices(sp, S, S.f2)
        chunks(sp, qb, chunk)

    q_blocks(sp, lambda qb: [step(qb, hg) for hg in range(NHG)])
    sp.wait_ge(a.st, 8 * index(NQB - 1, NHG - 1, NQB - 1))
    for par in range(2):
        sp.wait_ge(a.at_out[par], 16 * NHG)
    for G in range(2):
        load_attended(sp, S, G, G)
    load_gate_weights(sp, S, S.f2)


K_LOADS = 7


def load_keys(pool, S, kc):
    m, a = S.m, S.a
    if not (isinstance(kc, int) and kc == 0):
        pool.wait_ge(a.k_in, 16 * K_LOADS * kc)
    chunk = m.K[:, ds(kc * H * QB, H * QB)].rearrange("r (h t) -> r h t", h=H)
    for c, part in enumerate(K_PART):
        pool.dma_start(chunk[HD * c:HD * (c + 1)],
                       S.qk_d[1, part, :, ds(kc * QB, QB)].rearrange("(h d) t -> d h t", d=HD)).then_inc(a.k_in, 16)
    pool.dma_start(chunk[KR:KR + AR + MR],
                   S.ins["c_krows"][:, ds(kc * QB, QB)].unsqueeze(1).broadcast_to([AR + MR, H, QB])).then_inc(a.k_in, 16)


def store_heads(pool, S, qb, hg, s):
    m, a = S.m, S.a
    o = m.o[hg % 2]
    wait_alone(pool, S, a.o_copied, s)
    for j in range(HG):
        pool.dma_start(S.sums_d[j:j + 1, :], o[32 * j + HD:32 * j + HD + 1, :]).then_inc(a.sums_out, 16)
    wait_alone(pool, S, a.sums_out, 16 * HG * s)
    pool.dma_start(m.sums[:, :], S.sums_d.rearrange("j (b c) -> (j b) c", c=HG * QB // P)).then_inc(a.sums_in, 16)
    wait_alone(pool, S, a.recip, s)
    pool.dma_start(S.recips_d.rearrange("j (b c) -> (j b) c", c=HG * QB // P), m.recips[:, :]).then_inc(a.recips_out, 16)
    wait_alone(pool, S, a.recips_out, 16 * s)
    if not (isinstance(s, int) and s == 1):
        wait_alone(pool, S, a.normed, s - 1)
    for j in range(HG):
        pool.dma_start(m.rden[32 * j:32 * j + 32, :], S.recips_d[j:j + 1, :].broadcast_to([32, QB])).then_inc(a.recips_in, 16)
    wait_alone(pool, S, a.recips_in, 16 * HG * s)
    pool.tensor_tensor(o[:, :], o[:, :], m.rden[:, :], ALU.mult).then_inc(a.normed, 1)
    pool.wait_ge(a.normed, s)
    pool.dma_start(S.at_d[hg, :, ds(qb * QB, QB)], o[:, :]).then_inc(a.at_out[hg % 2], 16)


def attend_pool(pool, S):

    def block(qb):
        last = isinstance(qb, int) and qb == NQB - 1
        if not last:
            load_keys(pool, S, qb + 1)
        if not (isinstance(qb, int) and qb == 0):
            store_heads(pool, S, qb - 1, NHG - 1, NHG * qb)
        for hg in range(1, NHG):
            store_heads(pool, S, qb, hg - 1, NHG * qb + hg)
    q_blocks(pool, block)



def load_output_weights(sp, S):
    m, ins, s = S.m, S.ins, S.f2
    sp.wait_ge(s.wo_set, 1)
    wo = ins["WoT"].rearrange("(g j d) e -> j d g e", g=NHG, j=HG)
    for j in range(HG):
        sp.dma_start(m.wo_raw[32 * j:32 * j + HD, :].rearrange("p (g e) -> p g e", g=NHG), wo[j]).then_inc(s.wo_in, 16)
    sp.dma_start(m.wo_raw[HD:HD + 1, 0:D], ins["bo"].rearrange("(a n) -> a n", a=1)).then_inc(s.wo_in, 16)


def load_attended(sp, S, G, u):
    m, s = S.m, S.f2
    x_in = (s.x_in0, s.x_in1)
    at_in = (s.at_in0, s.at_in1)
    n = G // 2 if isinstance(G, int) else (G - u) // 2
    if isinstance(G, int) and G == 3:
        for par in range(2):
            sp.wait_ge(S.a.at_out[par], 16 * NHG * NQB // 2)
    if not (isinstance(G, int) and G < 2):
        sp.wait_ge(x_in[u], 16 * n)
        sp.wait_ge(at_in[u], 16 * n)
        sp.wait_ge(s.at_lo, NHG * (G - 1))
    sp.dma_start(m.at_raw[u][:, :].rearrange("p (g t) -> p g t", g=NHG),
                 S.at_d[:, :, ds(G * GW, GW)].rearrange("g p t -> p g t")).then_inc(at_in[u], 16)
    sp.dma_start(m.xs[:, ds(G * GT * D, GT * D)].rearrange("p (n d) -> p n d", d=D),
                 S.x1_d.rearrange("(n p) d -> p n d", p=P)[:, ds(G * GT, GT), :]).then_inc(x_in[u], 16)


def ffn2_dma(sp, S):
    store_groups(sp, S, S.f2, S.out, lambda G, u: load_attended(sp, S, G, u))


WO_LOADS = 16 * (HG + 1)


def ffn2_pe(pe, S):
    m, s = S.m, S.f2

    def attended(G, u):
        pe.wait_ge(s.at_lo, NHG * (G + 1))
        if not (isinstance(G, int) and G == 0):
            pe.wait_ge(s.lo, KD * G)
        if not (isinstance(G, int) and G == 0):
            pe.wait_ge(s.x2, G)
        for t in range(GT):
            last = split_product(pe, S.tb[t // 2][:, (t % 2) * D:(t % 2 + 1) * D],
                                 lambda g: m.at_hi[:, g * GW + t * P:g * GW + (t + 1) * P],
                                 lambda g: m.at_lo[:, g * GW + t * P:g * GW + (t + 1) * P],
                                 lambda g: m.wo_hi[:, g * D:(g + 1) * D], lambda g: m.wo_lo[:, g * D:(g + 1) * D], range(NHG))
        last.then_inc(s.attended, 1)

    pe.wait_ge(s.wo_lo, 1)
    attended(0, 0)
    ffn_pe(pe, S, s, lambda G: pe.wait_ge(s.x2, G + 1), attended, second=lambda: attended(1, 1))


def ffn2_act(act, S):
    m, s = S.m, S.f2
    at_in = (s.at_in0, s.at_in1)

    def at_hi(G, u):
        n = G // 2 if isinstance(G, int) else (G - u) // 2
        act.wait_ge(at_in[u], 16 * (n + 1))
        if not (isinstance(G, int) and G == 0):
            act.wait_ge(s.attended, G)
        act.activation(m.at_hi[:, :], m.at_raw[u][:, :], ACT.Copy).then_inc(s.at_hi, 1)
    for G in range(2):
        at_hi(G, G)
    norm_std_act(act, S, s, 0, 0)
    ffn_act(act, S, s, at_hi, lambda: norm_std_act(act, S, s, 1, 1))


def ffn2_dve(dve, S):
    m, s = S.m, S.f2
    x_in = (s.x_in0, s.x_in1)
    dve.sem_inc(s.used, E)
    dve.wait_ge(s.at_hi, 1)
    for g in range(NHG):
        c = slice(g * GW, (g + 1) * GW)
        dve.tensor_tensor(m.at_lo[:, c], m.at_raw[0][:, c], m.at_hi[:, c].bitcast(fp32), ALU.subtract).then_inc(s.at_lo, 1)
    dve.wait_ge(s.w_in, W_LOADS)
    dve.tensor_copy(m.g_hi[:, :], m.g_raw[:, :]).then_inc(s.w_hi, 1)
    split_gates(None, dve, S, s)

    def ready(G, u):
        n = G // 2 if isinstance(G, int) else (G - u) // 2
        dve.wait_ge(x_in[u], 16 * (n + 1))
        dve.wait_ge(s.attended, G + 1)
        for k in range(2):
            x = m.xs[:, ds((G * GT + 2 * k) * D, 2 * D)]
            ins = dve.tensor_tensor(x, x, S.tb[k][:, :], ALU.add)
        ins.then_inc(s.x2, 1)
        wait_alone(dve, S, s.x2, G + 1)

    def second():
        norm_stats_dve(dve, S, s, 1, 1, lambda: ready(1, 1))
        norm_apply_dve(dve, S, s, 1, 1)
        reciprocals_dve(dve, S, NHG * NQB)
    norm_stats_dve(dve, S, s, 0, 0, lambda: ready(0, 0))
    norm_apply_dve(dve, S, s, 0, 0)
    ffn_dve(dve, S, s, ready, second)


def ffn2_pool(pool, S):
    m, s = S.m, S.f2
    pool.sem_inc(s.added, 2)

    def at_lo(G, u, g):
        c = slice(g * GW, (g + 1) * GW)
        if g == 0:
            pool.wait_ge(s.at_hi, G + 1)
        pool.tensor_tensor(m.at_lo[:, c], m.at_raw[u][:, c], m.at_hi[:, c].bitcast(fp32), ALU.subtract).then_inc(s.at_lo, 1)
    for g in range(NHG):
        at_lo(1, 1, g)
    store_heads(pool, S, NQB - 1, NHG - 1, NHG * NQB)

    def also(G, u, t):
        if t < 2:
            at_lo(G, u, 2 * t)
            at_lo(G, u, 2 * t + 1)
    ffn_pool(pool, S, s, also)



def kernel(**inputs):
    import concourse.bacc as bacc
    from concourse.bass_utils import run_bass_kernel_spmd as run

    def arr(name):
        return np.ascontiguousarray(inputs[name])

    arrays = {
        "x": arr("L0_attn_x").reshape(L, D),
        "WqT": np.ascontiguousarray(arr("L0_attn_Wq").T), "bq": arr("L0_attn_bq"),
        "WkT": np.ascontiguousarray(arr("L0_attn_Wk").T), "bk": arr("L0_attn_bk"),
        "WvT": np.ascontiguousarray(arr("L0_attn_Wv").T), "bv": arr("L0_attn_bv"),
        "WoT": np.ascontiguousarray(arr("L0_attn_Wo").T), "bo": arr("L0_attn_bo"),
        "gate_wT": np.ascontiguousarray(arr("L0_ffn_gate_w").T), "gate_b": arr("L0_ffn_gate_b"),
        "expert_w": arr("L0_ffn_expert_w"), "expert_b": arr("L0_ffn_expert_b"),
    }
    arrays.update(constant_arrays())
    nc = bacc.Bacc("TRN2", target_bir_lowering=False, num_devices=1)
    ins = {n: nc.dram_tensor(n, v.shape, mybir.dt.from_np(v.dtype), kind="ExternalInput").ap() for n, v in arrays.items()}
    ins = {n: v.bitcast(bf16) if arrays[n].dtype == np.uint16 else v for n, v in ins.items()}
    out = nc.dram_tensor("out", [L, D], fp32, kind="ExternalOutput").ap()
    program(nc, ins, out)
    r = run(nc, [arrays], core_ids=[0])
    return r.results[0]["out"].reshape(1, L, D)
```
